# Optimizing a Trainium2 kernel written in Bass

```python
import numpy as np
import jax
import jax.numpy as jnp

def _softmax(x, axis=-1):
    return jax.nn.softmax(x, axis=axis)

def _gelu(x):
    return jax.nn.gelu(x, approximate=True)

def _silu(x):
    return jax.nn.silu(x)

def _sigmoid(x):
    return jax.nn.sigmoid(x)

def _layernorm(x, axis=-1, eps=1e-05):
    m = jnp.mean(x, axis=axis, keepdims=True)
    v = jnp.var(x, axis=axis, keepdims=True)
    return (x - m) / jnp.sqrt(v + eps)

def _scatter_add(tgt, idx, src, axis=0):
    return tgt.at[idx].add(src)

def _segment_sum(src, seg, n):
    return jax.ops.segment_sum(src, seg, n)
kernel_name = 'mk_gnn_ffn_d1_gnn_r8_90c850'

def setup_inputs(seed: int=0):
    np.random.seed(seed)
    _w = jnp.asarray

    def _rec_inputs():
        import jax
        import jax.numpy as jnp
        _gk = jax.random.key(seed)
        x = -0.0001126 + 1 * jax.random.normal(jax.random.fold_in(_gk, 1), (1250, 768), jnp.float32)
        src = jax.random.randint(jax.random.fold_in(_gk, 2), (40000,), 0, 1250, jnp.int32)
        dst = jax.random.randint(jax.random.fold_in(_gk, 3), (40000,), 0, 1250, jnp.int32)
        _o = jnp.argsort(dst, stable=True)
        src = src[_o]
        dst = dst[_o]
        return (x, src, dst)
    x, src, dst = _rec_inputs()

    def _L0_gnn_setup():
        import jax, jax.numpy as jnp
        import numpy as np
        N_NODES = 1250
        N_EDGES = 12500
        DIM = 768
        NEG_SLOPE = 0.2

        def gat_conv(x, src, dst, W, att_src, att_dst, bias, num_nodes):
            h = x @ W
            a_s = h @ att_src
            a_d = h @ att_dst
            e = jax.nn.leaky_relu(a_s[src] + a_d[dst], NEG_SLOPE)
            m = jax.ops.segment_max(e, dst, num_segments=num_nodes)
            e = jnp.exp(e - m[dst])
            denom = jax.ops.segment_sum(e, dst, num_segments=num_nodes)
            alpha = e / denom[dst]
            msg = alpha[:, None] * h[src]
            out = jax.ops.segment_sum(msg, dst, num_segments=num_nodes)
            return out + bias
        key = jax.random.key(seed)
        ks = jax.random.split(key, 12)
        s = 1.0 / np.sqrt(DIM)
        inp = {'x': jax.random.normal(ks[0], (N_NODES, DIM), dtype=jnp.float32), 'edge_index': jax.random.randint(ks[1], (2, N_EDGES), 0, N_NODES, dtype=jnp.int64), 'W1': jax.random.normal(ks[2], (DIM, DIM), dtype=jnp.float32) * s, 'att_src1': jax.random.normal(ks[3], (DIM,), dtype=jnp.float32) * s, 'att_dst1': jax.random.normal(ks[4], (DIM,), dtype=jnp.float32) * s, 'b1': jnp.zeros((DIM,), dtype=jnp.float32), 'W2': jax.random.normal(ks[5], (DIM, DIM), dtype=jnp.float32) * s, 'att_src2': jax.random.normal(ks[6], (DIM,), dtype=jnp.float32) * s, 'att_dst2': jax.random.normal(ks[7], (DIM,), dtype=jnp.float32) * s, 'b2': jnp.zeros((DIM,), dtype=jnp.float32)}
        return inp
    _L0_gnn_all = _L0_gnn_setup()
    _L0_gnn_in = {k: v for k, v in _L0_gnn_all.items() if k in ('W1', 'att_src1', 'att_dst1', 'b1', 'W2', 'att_src2', 'att_dst2', 'b2')}
    del _L0_gnn_all

    def _L0_ffn_setup():
        import jax, jax.numpy as jnp
        import numpy as np
        import math
        B, T, C = (8, 256, 768)
        E = 3
        HD = C // E
        TOPK = 2
        NGLOB = 4

        def _masked_softmax(att, mask):
            att = jnp.where(mask, -jnp.inf, att)
            return jax.nn.softmax(att, axis=-1)
        key = jax.random.key(seed)
        ks = jax.random.split(key, 16)
        s = 0.02
        return {'x': jax.random.normal(ks[0], (B, T, C), jnp.float32), 'Wqk': jax.random.normal(ks[1], (C, 2 * C), jnp.float32) * s, 'bqk': jnp.zeros((2 * C,), jnp.float32), 'Wv': jax.random.normal(ks[2], (E, C, HD), jnp.float32) * s, 'bv': jnp.zeros((E, HD), jnp.float32), 'conv_w': jax.random.normal(ks[3], (HD, 1, 3), jnp.float32) * s, 'conv_b': jnp.zeros((HD,), jnp.float32), 'glob': jax.random.normal(ks[4], (NGLOB, HD), jnp.float32) * 0.02, 'pos_bias': jnp.zeros((64, 64), jnp.float32), 'Wg1': jax.random.normal(ks[5], (C, 32), jnp.float32) * s, 'bg1': jnp.zeros((32,), jnp.float32), 'Wg2': jax.random.normal(ks[6], (32, E), jnp.float32) * s, 'bg2': jnp.zeros((E,), jnp.float32), 'Wp': jax.random.normal(ks[7], (C, C), jnp.float32) * s, 'bp': jnp.zeros((C,), jnp.float32)}
    _L0_ffn_all = _L0_ffn_setup()
    _L0_ffn_in = {k: v for k, v in _L0_ffn_all.items() if k in ('Wqk', 'bqk', 'Wv', 'bv', 'conv_w', 'conv_b', 'glob', 'pos_bias', 'Wg1', 'bg1', 'Wg2', 'bg2', 'Wp', 'bp')}
    del _L0_ffn_all
    return {'x': x, 'src': src, 'dst': dst, 'L0_gnn_W1': _L0_gnn_in['W1'], 'L0_gnn_att_src1': _L0_gnn_in['att_src1'], 'L0_gnn_att_dst1': _L0_gnn_in['att_dst1'], 'L0_gnn_b1': _L0_gnn_in['b1'], 'L0_gnn_W2': _L0_gnn_in['W2'], 'L0_gnn_att_src2': _L0_gnn_in['att_src2'], 'L0_gnn_att_dst2': _L0_gnn_in['att_dst2'], 'L0_gnn_b2': _L0_gnn_in['b2'], 'L0_ffn_Wqk': _L0_ffn_in['Wqk'], 'L0_ffn_bqk': _L0_ffn_in['bqk'], 'L0_ffn_Wv': _L0_ffn_in['Wv'], 'L0_ffn_bv': _L0_ffn_in['bv'], 'L0_ffn_conv_w': _L0_ffn_in['conv_w'], 'L0_ffn_conv_b': _L0_ffn_in['conv_b'], 'L0_ffn_glob': _L0_ffn_in['glob'], 'L0_ffn_pos_bias': _L0_ffn_in['pos_bias'], 'L0_ffn_Wg1': _L0_ffn_in['Wg1'], 'L0_ffn_bg1': _L0_ffn_in['bg1'], 'L0_ffn_Wg2': _L0_ffn_in['Wg2'], 'L0_ffn_bg2': _L0_ffn_in['bg2'], 'L0_ffn_Wp': _L0_ffn_in['Wp'], 'L0_ffn_bp': _L0_ffn_in['bp']}

def reference(x, src, dst, L0_gnn_W1, L0_gnn_att_src1, L0_gnn_att_dst1, L0_gnn_b1, L0_gnn_W2, L0_gnn_att_src2, L0_gnn_att_dst2, L0_gnn_b2, L0_ffn_Wqk, L0_ffn_bqk, L0_ffn_Wv, L0_ffn_bv, L0_ffn_conv_w, L0_ffn_conv_b, L0_ffn_glob, L0_ffn_pos_bias, L0_ffn_Wg1, L0_ffn_bg1, L0_ffn_Wg2, L0_ffn_bg2, L0_ffn_Wp, L0_ffn_bp):
    import jax
    import jax.numpy as jnp

    def _L0_gnn_ref(x, edge_index, W1, att_src1, att_dst1, b1, W2, att_src2, att_dst2, b2):
        import jax, jax.numpy as jnp
        import numpy as np
        N_NODES = 1250
        N_EDGES = 12500
        DIM = 768
        NEG_SLOPE = 0.2

        def gat_conv(x, src, dst, W, att_src, att_dst, bias, num_nodes):
            h = x @ W
            a_s = h @ att_src
            a_d = h @ att_dst
            e = jax.nn.leaky_relu(a_s[src] + a_d[dst], NEG_SLOPE)
            m = jax.ops.segment_max(e, dst, num_segments=num_nodes)
            e = jnp.exp(e - m[dst])
            denom = jax.ops.segment_sum(e, dst, num_segments=num_nodes)
            alpha = e / denom[dst]
            msg = alpha[:, None] * h[src]
            out = jax.ops.segment_sum(msg, dst, num_segments=num_nodes)
            return out + bias
        n = x.shape[0]
        loops = jnp.arange(n, dtype=edge_index.dtype)
        src = jnp.concatenate([edge_index[0], loops])
        dst = jnp.concatenate([edge_index[1], loops])
        h = gat_conv(x, src, dst, W1, att_src1, att_dst1, b1, n)
        h = jax.nn.relu(h)
        out = gat_conv(h, src, dst, W2, att_src2, att_dst2, b2, n)
        return out

    def _L0_ffn_ref(x, Wqk, bqk, Wv, bv, conv_w, conv_b, glob, pos_bias, Wg1, bg1, Wg2, bg2, Wp, bp):
        import jax, jax.numpy as jnp
        import numpy as np
        import math
        B, T, C = (8, 256, 768)
        E = 3
        HD = C // E
        TOPK = 2
        NGLOB = 4

        def _masked_softmax(att, mask):
            att = jnp.where(mask, -jnp.inf, att)
            return jax.nn.softmax(att, axis=-1)
        Bx, Tx, Cx = x.shape
        scale = 1.0 / math.sqrt(HD)
        gate = jax.nn.softmax(jax.nn.relu(x @ Wg1 + bg1) @ Wg2 + bg2, axis=-1)
        top_w, top_i = jax.lax.top_k(gate, TOPK)
        top_w = jax.nn.softmax(top_w, axis=-1)
        qk = x @ Wqk + bqk
        q, k = (qk[..., :Cx], qk[..., Cx:])
        q = q.reshape(Bx, Tx, E, HD)
        k = k.reshape(Bx, Tx, E, HD)
        rows = jnp.arange(Tx)[:, None]
        ys = []
        for e in range(E):
            qe = q[:, :, e]
            ke = k[:, :, e]
            ve = x @ Wv[e] + bv[e]
            if e == 0:
                qc = jnp.transpose(qe, (0, 2, 1))
                qc = jax.lax.conv_general_dilated(qc, conv_w, window_strides=(1,), padding=((1, 1),), feature_group_count=HD, dimension_numbers=('NCH', 'OIH', 'NCH'))
                qe = jnp.transpose(qc + conv_b[None, :, None], (0, 2, 1))
            elif e == 1:
                gb = jnp.broadcast_to(glob[None], (Bx, NGLOB, HD))
                ke = jnp.concatenate([ke, gb], axis=1)
                ve = jnp.concatenate([ve, gb], axis=1)
            att = jnp.einsum('btd,bsd->bts', qe, ke) * scale
            if e == 2 and Tx <= 64:
                att = att + pos_bias[:Tx, :Tx][None]
            S = att.shape[-1]
            mask = jnp.arange(S)[None, :] > rows
            att = _masked_softmax(att, mask[None])
            ys.append(jnp.einsum('bts,bsd->btd', att, ve))
        ys = jnp.stack(ys, axis=2)
        w_e = jnp.sum(jax.nn.one_hot(top_i, E, dtype=x.dtype) * top_w[..., None], axis=-2)
        combined = (ys * w_e[..., None]).reshape(Bx, Tx, Cx)
        return combined @ Wp + bp
    edge_index = jnp.stack([src, dst])
    x = x + _L0_gnn_ref(_layernorm(x, axis=-1), edge_index, L0_gnn_W1, L0_gnn_att_src1, L0_gnn_att_dst1, L0_gnn_b1, L0_gnn_W2, L0_gnn_att_src2, L0_gnn_att_dst2, L0_gnn_b2)
    x = x + _L0_ffn_ref(_layernorm(x, axis=-1)[None], L0_ffn_Wqk, L0_ffn_bqk, L0_ffn_Wv, L0_ffn_bv, L0_ffn_conv_w, L0_ffn_conv_b, L0_ffn_glob, L0_ffn_pos_bias, L0_ffn_Wg1, L0_ffn_bg1, L0_ffn_Wg2, L0_ffn_bg2, L0_ffn_Wp, L0_ffn_bp)[0]
    return x

_drawn_inputs = setup_inputs


def setup_inputs(seed=0):
    import zlib

    import numpy as np

    out = dict(_drawn_inputs(seed))
    spreads = {'L0_gnn_b1': (0.0, 0.1),
     'L0_gnn_b2': (0.0, 0.1),
     'L0_ffn_bqk': (0.0, 0.8),
     'L0_ffn_bv': (0.0, 0.357),
     'L0_ffn_conv_b': (0.0, 0.8),
     'L0_ffn_pos_bias': (0.0, 0.1),
     'L0_ffn_bg1': (0.0, 0.8),
     'L0_ffn_bg2': (0.0, 0.292),
     'L0_ffn_bp': (0.0, 0.1)}
    factors = {'L0_gnn_att_dst1': 8.0,
     'L0_gnn_att_src2': 8.0,
     'L0_gnn_att_dst2': 64.0,
     'L0_ffn_Wqk': 8.0,
     'L0_ffn_Wv': 2.764,
     'L0_ffn_conv_w': 8.0,
     'L0_ffn_Wg1': 6.641,
     'L0_ffn_Wg2': 7.337}
    for name, (base, spread) in spreads.items():
        noise = np.random.default_rng([zlib.crc32(name.encode()), seed]).standard_normal(out[name].shape)
        drawn = base * np.exp(spread * noise) if base else spread * noise
        out[name] = jnp.asarray(drawn.astype(out[name].dtype))
    for name, factor in factors.items():
        out[name] = (out[name] * factor).astype(out[name].dtype)
    return out
```

```python
import numpy as np
import concourse.bass as bass
from concourse import mybir
from contextlib import ExitStack

F32 = mybir.dt.float32
F32R = mybir.dt.float32r
BF16 = mybir.dt.bfloat16
FP16 = mybir.dt.float16
I32 = mybir.dt.int32
U16 = mybir.dt.uint16
BYTES = {F32: 4, F32R: 4, I32: 4, BF16: 2, FP16: 2, U16: 2}
ALU = mybir.AluOpType
ACT = mybir.ActivationFunctionType
AX = mybir.AxisListType

N = 1250
E = 40000
D = 768
HEADS = 3
HD = D // HEADS
GATE = 32
T = 125
NT = N // T
P = 128
KC = D // P
HALF = D // 2
HC = HD // P
G = 80
GE = E // G
ET = GE // T
W = 24
WP = (N + W - 1) // W
CTW = N + W
PER_TILE = G // NT
OHS = T + T % 2
RING = 4
LAG = RING - 1
WX = D + 2
LN_EPS = 1e-5
NEG_SLOPE = 0.2
FAR = -1e30
ROUND = 12582912.0
WB = HD
WG = WB + GATE
BLOCKS = 3 * HEADS
SPAN = ((0, 418), (418, 416), (834, 416))
BANK = 512
SCALE = HD ** -0.5
PARTS = ((1, 0), (0, 1), (0, 0))
HIGH_FIRST = ((0, 0), (0, 1), (1, 0))


class Own:

    def __init__(self, eng, sem):
        self.eng, self.sem, self.base, self.n = eng, sem, 0, 0

    def mark(self, ins):
        ins.then_inc(self.sem, 1)
        self.n += 1

    def wait(self):
        self.eng.wait_ge(self.sem, self.base + self.n)

    def done(self, ins):
        self.mark(ins)
        self.wait()

    def enter(self, i, steps):
        kept = (self.base, self.n, steps)
        self.base, self.n = self.base + self.n + i * steps, 0
        return kept

    def leave(self, kept, times):
        base, n, steps = kept
        assert self.n == steps, (self.n, steps)
        self.base, self.n = base, n + times * steps


def program(nc, x, src, dst, gnn, ffn, out):
    ctx = ExitStack()
    with ctx:
        def sem(name):
            return ctx.enter_context(nc.semaphore(name))

        BASE, TOP = 16512, 229368
        tensors = {}

        def sb(name, shape, dt, offset):
            size = int(np.prod(shape[1:])) * BYTES[dt]
            assert offset % 4 == 0 and BASE + offset + size <= TOP, (name, offset, size)
            tensors[name] = (offset, size)
            return nc.alloc_sbuf_tensor_at(name, shape, dt, offset=BASE + offset)

        def after(name):
            o, s = tensors[name]
            return (o + s + 31) // 32 * 32

        ident = sb("ident", [P, P], F32, 0)
        ones = sb("ones", [P, P], F32, after("ident"))
        gate_scale = sb("gate_scale", [T, HEADS, NT], F32, after("ones"))
        asd = sb("asd", [T, NT, 2], F32, after("gate_scale"))
        small = sb("small", [P, 64], F32, after("asd"))
        flag = sb("flag", [1, 1], I32, after("small"))
        H = [sb("H_hi", [T, NT, D], F32R, after("flag")), None]
        H[1] = sb("H_lo", [T, NT, D], F32R, after("H_hi"))
        counts = sb("counts", [T, NT, N], U16, after("H_lo"))
        Wg = [sb("W_hi", [P, KC, WX], F32R, after("counts")), None]
        Wg[1] = sb("W_lo", [P, KC, WX], F32R, after("W_hi"))
        XT = [sb("XT_hi", [P, KC, T], F32R, after("W_lo")), None]
        XT[1] = sb("XT_lo", [P, KC, T], F32R, after("XT_hi"))
        Wraw = sb("Wraw", [P, KC, WX], F32, tensors["counts"][0])

        xall = sb("xall", [T, NT, D], F32, after("XT_lo"))
        xn = sb("xn", [T, D], F32, after("xall"))
        xt_raw = sb("xt_raw", [P, KC, T], F32, after("xn"))
        h_raw = sb("h_raw", [T, WX], F32, after("xt_raw"))
        bn = sb("bn", [T, NT, 2, 6], F32, after("h_raw"))
        mv = sb("mv", [T, NT, 2], F32, after("bn"))
        rstd = sb("rstd", [T, NT], F32, after("mv"))
        negmean = sb("negmean", [T, NT], F32, after("rstd"))
        varep = sb("varep", [T, NT], F32, after("negmean"))
        shift = sb("shift", [T, NT], F32, after("varep"))
        minus_half = sb("minus_half", [T, NT], F32, after("shift"))
        oh_src = sb("oh_src", [T, RING, ET, OHS], BF16, after("minus_half"))
        oh_win = sb("oh_win", [T, RING, ET, NT * W], BF16, after("oh_src"))
        countsT = sb("countsT", [T, NT, CTW], U16, after("oh_win"))
        iota = sb("iota", [T, NT * W], FP16, after("countsT"))
        bases = sb("bases", [1, G], I32, after("iota"))
        tab_low = sb("tab_low", [T, G, ET, 2], FP16, after("Wraw"))
        tab_win = sb("tab_win", [T, G, ET, 2], FP16, after("tab_low"))
        tab_dst = sb("tab_dst", [T, ET, G], F32, after("tab_win"))
        tab_high = sb("tab_high", [T, ET, G], F32, after("tab_dst"))
        e0 = tensors["H_hi"][0]
        dst_i = sb("dst_i", [G, GE], I32, e0)
        src_i = sb("src_i", [G, GE], I32, e0 + 4096)
        dst_f = sb("dst_f", [G, GE], F32, e0 + 2 * 4096)
        src_high = sb("src_high", [G, GE], F32, e0 + 3 * 4096)
        src_low = sb("src_low", [G, GE], F32, e0 + 4 * 4096)
        rel = sb("rel", [G, GE], F32, e0 + 5 * 4096)
        win = sb("win", [G, GE], F32, e0 + 6 * 4096)
        iota_i = sb("iota_i", [T, NT * W], I32, e0 + 7 * 4096)
        attb = sb("attb", [P, 2, D], F32, e0 + 8 * 4096)
        junk_w = sb("junk_w", [P, D], F32, e0 + 10 * 4096)
        tab_rel = sb("tab_rel", [T, ET, G], F32, tensors["xn"][0])
        tab_ok = sb("tab_ok", [T, ET, G], F32, after("tab_rel"))
        tab_to = sb("tab_to", [T, ET, G], F32, tensors["xt_raw"][0])
        ct_f = sb("ct_f", [T, 2, NT, T], F32, tensors["oh_src"][0])

        Wraw2 = sb("Wraw2", [P, KC, WX], F32, tensors["xall"][0])
        attb2 = sb("attb2", [P, 2, D], F32, after("Wraw2"))
        product = sb("product", [P, D], F32, after("attb2"))
        h_next = sb("h_next", [T, NT, D], F32, tensors["xall"][0])
        asb = sb("asb", [T, NT, T], F32, after("xall"))
        prob = sb("prob", [T, N], F32, after("asb"))
        far = sb("far", [T, N], BF16, after("prob"))
        junk = sb("junk", [T, N], BF16, after("far"))
        PT = [sb("PT_hi", [T, NT, T], F32R, after("junk")), None]
        PT[1] = sb("PT_lo", [T, NT, T], F32R, after("PT_hi"))
        rows = sb("rows", [T, D], F32, after("PT_lo"))
        bias_b = sb("bias_b", [T, D], F32, after("rows"))
        ad_slope = sb("ad_slope", [T, NT], F32, after("bias_b"))
        rden = sb("rden", [T, NT], F32, after("ad_slope"))
        stat = sb("stat", [T, 8], F32, after("rden"))
        diag = sb("diag", [T, NT, T], F32, after("stat"))
        xnT = [sb("xnT_hi", [P, KC, N], F32R, tensors["W_hi"][0]), None]
        xnT[1] = sb("xnT_lo", [P, KC, N], F32R, after("xnT_hi"))
        x_plus = sb("x_plus", [T, D], F32, after("xnT_lo"))
        xn2 = sb("xn2", [T, D], F32, after("x_plus"))
        bn2 = sb("bn2", [T, 2, 6], F32, after("xn2"))
        mv2 = sb("mv2", [T, 2], F32, after("bn2"))
        ln2 = sb("ln2", [T, 4], F32, after("mv2"))
        half2 = sb("half2", [T, 1], F32, after("ln2"))
        assert after("half2") <= tensors["asb"][0]

        qT = [sb("qT_hi", [P, HC, N], F32R, tensors["H_hi"][0]), None]
        qT[1] = sb("qT_lo", [P, HC, N], F32R, after("qT_hi"))
        kT = [sb("kT_hi", [P, HC, N], F32R, after("qT_lo")), None]
        kT[1] = sb("kT_lo", [P, HC, N], F32R, after("kT_hi"))
        vs = [sb("v_hi", [T, NT, HD], F32R, after("kT_lo")), None]
        vs[1] = sb("v_lo", [T, NT, HD], F32R, after("v_hi"))
        q_raw = sb("q_raw", [P, HC, N + 2], F32, after("v_lo"))
        tri = sb("tri", [T, T], F32, after("q_raw"))
        bqk_c = sb("bqk_c", [P, 2 * KC], F32, after("tri"))
        conv_wc = sb("conv_wc", [P, HC, 3], F32, after("bqk_c"))
        conv_bc = sb("conv_bc", [P, HC], F32, after("conv_wc"))
        bg1_b = sb("bg1_b", [T, GATE], F32, after("conv_bc"))
        bg2_b = sb("bg2_b", [T, HEADS], F32, after("bg1_b"))
        wg2_b = sb("wg2_b", [T, GATE, HEADS], F32, after("bg2_b"))
        bv_b = sb("bv_b", [T, D], F32, after("wg2_b"))
        gate_h = sb("gate_h", [T, NT, GATE], F32, after("bv_b"))
        gate_t = sb("gate_t", [T, NT, GATE], F32, after("gate_h"))
        gate_e = sb("gate_e", [T, HEADS, NT], F32, after("gate_t"))
        gate_c = sb("gate_c", [T, 4, NT], F32, after("gate_e"))
        att_max = sb("att_max", [T, 4], F32, after("gate_c"))
        att_den = sb("att_den", [T, 4], F32, after("att_max"))
        ys_out = sb("ys_out", [T, 2, HD], F32, after("att_den"))
        assert after("ys_out") <= tensors["xnT_hi"][0]
        pexp = sb("pexp", [P, N], F32, after("xnT_lo"))
        w_raw = sb("w_raw", [P, KC, WG], F32, after("half2"))
        Ws = [[None] * 3, [None] * 3]
        Ws[0][1] = sb("Ws_k_hi", [P, KC, WB], F32R, after("w_raw"))
        Ws[1][1] = sb("Ws_k_lo", [P, KC, WB], F32R, after("Ws_k_hi"))
        Ws[0][2] = sb("Ws_v_hi", [P, KC, WG], F32R, after("Ws_k_lo"))
        Ws[1][2] = sb("Ws_v_lo", [P, KC, WG], F32R, after("Ws_v_hi"))
        pT = [sb("pT_hi", [T, NT, T], F32R, after("Ws_v_lo")), None]
        pT[1] = sb("pT_lo", [T, NT, T], F32R, after("pT_hi"))
        Ws[0][0] = sb("Ws_q_hi", [P, KC, WB], F32R, max(after("pT_lo"), after("diag")))
        Ws[1][0] = sb("Ws_q_lo", [P, KC, WB], F32R, after("Ws_q_hi"))
        assert after("pexp") <= tensors["w_raw"][0] and after("w_raw") <= tensors["asb"][0]
        yT = [sb("yT_hi", [P, 2, KC, T], F32R, tensors["qT_hi"][0]), None]
        yT[1] = sb("yT_lo", [P, 2, KC, T], F32R, after("yT_hi"))
        y_in = sb("y_in", [T, 2, D], F32, after("yT_lo"))
        x2_in = sb("x2_in", [T, 2, D], F32, after("y_in"))
        out_sb = sb("out_sb", [T, 2, D], F32, after("x2_in"))
        bp_b = sb("bp_b", [T, D], F32, after("out_sb"))
        assert after("bp_b") <= tensors["v_hi"][0]

        PS = ctx.enter_context(nc.psum_tensor("PS", [P, 8, 512], F32))

        def blocks(bank, n):
            return PS[:, bank:bank + (n + 3) // 4, :].rearrange("p b (q c) -> p (b q) c", c=P)[:, 0:n, :]

        def bank(b, rows, cols):
            return PS[0:rows, b, 0:cols]

        edges_in, bases_in, x_in, w_in, att_in = (sem(s) for s in
            ("edges_in", "bases_in", "x_in", "w_in", "att_in"))
        dve_counts = sem("dve_counts")
        pool_own, dve_own, act_own = sem("pool_own"), sem("dve_own"), sem("act_own")
        consts_ready = sem("consts_ready")
        edge_rows_ready, edge_rows_turned, tables_ready = sem("edge_rows_ready"), sem("edge_rows_turned"), sem("tables_ready")
        stats_ready, scale_ready = sem("stats_ready"), sem("scale_ready")
        att_cols_ready = sem("att_cols_ready")
        w_hi_ready, w_lo_ready = sem("w_hi_ready"), sem("w_lo_ready")
        xn_ready, xn_turned, xt_raw_ready, xt_hi_ready, xt_lo_ready = (sem(s) for s in
            ("xn_ready", "xn_turned", "xt_raw_ready", "xt_hi_ready", "xt_lo_ready"))
        h_free = sem("h_free")
        h_done, h_hi_ready, h_lo_ready = (sem(s) for s in
            ("h_done", "h_hi_ready", "h_lo_ready"))
        onehots_ready, group_counted, window_free = (sem(s) for s in
            ("onehots_ready", "group_counted", "window_free"))
        countsT_zero, countsT_ready = sem("countsT_zero"), sem("countsT_ready")
        ct_conv, ct_diag, ct_turned, counts_ready = (sem(s) for s in
            ("ct_conv", "ct_diag", "ct_turned", "counts_ready"))
        out_in = sem("out_in")
        w2_in, att2_in, att2_cols, w2_hi, w2_lo = (sem(s) for s in
            ("w2_in", "att2_in", "att2_cols", "w2_hi", "w2_lo"))
        split_hi, split_dve, split_pool = (sem(s) for s in ("split_hi", "split_dve", "split_pool"))
        half_ready, x_again, x_plus_ready, x2_stored, var_ready, ln_ready, xn2_ready = (sem(s) for s in
            ("half_ready", "x_again", "x_plus_ready", "x2_stored", "var_ready", "ln_ready", "xn2_ready"))
        LAYER = [{name: sem(f"{name}_{l}") for name in (
            "bias_in", "diag_ready", "asb_turned", "asb_ready", "line_ready", "arg_ready", "exp_ready",
            "probs_ready", "probs_turned", "pt_hi", "pt_lo", "rows_done", "rows_out", "rows_turned",
            "xt_hi", "xt_lo", "msgs_done", "msgs_out")} for l in range(2)]
        ws_in, ws_hi, ws_lo, tabs_in, tri_ready = (sem(s) for s in ("ws_in", "ws_hi", "ws_lo", "tabs_in", "tri_ready"))
        group_done, group_hi, group_free, conv_ready, conv_hi = (sem(s) for s in
            ("group_done", "group_hi", "group_free", "conv_ready", "conv_hi"))
        scores_done, max_ready, pexp_ready, pexp_turned, pexp_hi, pexp_lo = (sem(s) for s in
            ("scores_done", "max_ready", "pexp_ready", "pexp_turned", "pexp_hi", "pexp_lo"))
        gate_arg, gate_exp, gate_ready = (sem(s) for s in ("gate_arg", "gate_exp", "gate_ready"))
        ys_stored = [sem("ys_stored_even"), sem("ys_stored_odd")]
        y_loaded = [sem("y_loaded_even"), sem("y_loaded_odd")]
        x2_loaded = [sem("x2_loaded_even"), sem("x2_loaded_odd")]
        out_stored = [sem("out_stored_even"), sem("out_stored_odd")]
        bp_in, y_scaled, y_turned, yt_hi, yt_lo, x2_plus, proj_done, out_ready = (sem(s) for s in
            ("bp_in", "y_scaled", "y_turned", "yt_hi", "yt_lo", "x2_plus", "proj_done", "out_ready"))
        y_dram = nc.dram_tensor("y_scratch", [N, D], F32).ap()
        x2_dram = nc.dram_tensor("x2_scratch", [N, D], F32).ap()

        block = ctx.enter_context(nc.Block())

        def rows_in(eng, to, frm, s):
            eng.dma_start(to[0:120], frm[0:120]).then_inc(s, 16)
            eng.dma_start(to[120:T], frm[120:T]).then_inc(s, 16)

        def rows_out_to(eng, to, frm, s):
            eng.dma_start(to[0:120], frm[0:120, :]).then_inc(s, 16)
            eng.dma_start(to[120:T], frm[120:T, :]).then_inc(s, 16)

        def act_line(l, d):
            L = LAYER[l]
            if not isinstance(d, int) or d >= 1:
                nc.scalar.wait_ge(L["probs_turned"], d)
            nc.scalar.activation(prob[:, :], asb[:, :, :].rearrange("p a b -> p (a b)"), ACT.Identity,
                                 bias=ad_slope[:, bass.ds(d, 1)], scale=NEG_SLOPE).then_inc(L["line_ready"], 1)
            nc.scalar.wait_ge(L["arg_ready"], d + 1)
            nc.scalar.activation(prob[:, :], prob[:, :], ACT.Exp).then_inc(L["exp_ready"], 1)

        def act_probs_high(l, d):
            L = LAYER[l]
            nc.scalar.wait_ge(L["probs_turned"], d + 1)
            nc.scalar.activation(PT[0][:, :, :], blocks(0, NT)[0:T, :, 0:T], ACT.Copy).then_inc(L["pt_hi"], 1)

        def act_rows_high(l, d):
            L = LAYER[l]
            if l == 0:
                nc.scalar.wait_ge(L["rows_turned"], d + 1)
                nc.scalar.activation(XT[0][:, :, :], blocks(0, KC)[:, :, 0:T], ACT.Relu).then_inc(L["xt_hi"], 1)
            else:
                nc.scalar.wait_ge(L["rows_turned"], d + 1)
                nc.scalar.activation(xnT[0][:, :, bass.ds(d * T, T)], blocks(row_bank(l, d), KC)[:, :, 0:T], ACT.Copy).then_inc(L["xt_hi"], 1)

        def act_normalise(d):
            nc.scalar.wait_ge(ln_ready, d + 1)
            nc.scalar.activation(xn2[:, :], rows[:, :], ACT.Identity, bias=ln2[:, 3:4], scale=ln2[:, 2:3]).then_inc(xn2_ready, 1)

        def act_messages_next(l, d):
            L = LAYER[l]
            if l == 0:
                nc.scalar.wait_ge(L["msgs_done"], d + 1)
                to = h_next[:, bass.ds(d, 1), :].rearrange("p a d -> p (a d)")
                nc.scalar.activation(to[:, 0:HALF], bank(5, T, HALF), ACT.Copy)
                nc.scalar.activation(to[:, HALF:D], bank(6, T, HALF), ACT.Copy)
                nc.scalar.activation(asd[:, bass.ds(d, 1), :].rearrange("p a b -> p (a b)"), PS[0:T, 6, HALF:HALF + 2], ACT.Copy).then_inc(L["msgs_out"], 1)

        def act_attention(l):
            L = LAYER[l]
            act = nc.scalar
            if l == 0:
                act.wait_ge(h_lo_ready, NT)
            act.wait_ge(L["asb_turned"], 1)
            act.activation(asb[:, :, :], blocks(0, NT)[0:T, :, 0:T], ACT.Copy).then_inc(L["asb_ready"], 1)
            act.wait_ge(L["asb_ready"], 1)
            act_line(l, 0)
            act_probs_high(l, 0)
            act_line(l, 1)
            act_probs_high(l, 1)
            act_line(l, 2)
            if l == 0:
                act.wait_ge(att2_cols, 1)
                act.activation(Wg[0][:, :, :], Wraw2[:, :, :], ACT.Copy).then_inc(w2_hi, 1)
                act_rows_high(l, 0)
                with act.Fori(1, NT - 2) as d:
                    act_probs_high(l, d + 1)
                    act_line(l, d + 2)
                    act_messages_next(l, d - 1)
                    act_rows_high(l, d)
                act_probs_high(l, NT - 1)
                for d in (NT - 2, NT - 1):
                    act_messages_next(l, d - 1)
                    act_rows_high(l, d)
                act_messages_next(l, NT - 1)
            else:
                act_normalise(0)
                act_weight(0)
                with act.Fori(1, NT - 2) as d:
                    act_probs_high(l, d + 1)
                    act_line(l, d + 2)
                    act_rows_high(l, d - 1)
                    act_normalise(d)
                act_probs_high(l, NT - 1)
                for d in (NT - 2, NT - 1):
                    act_rows_high(l, d - 1)
                    act_normalise(d)

        def dve_probs(l, d, own, stats_of=None):
            L, dve = LAYER[l], nc.vector
            cnt = counts[:, bass.ds(d, 1), :].rearrange("p a b -> p (a b)")
            ad = asd[:, bass.ds(d, 1), 1:2].rearrange("p a b -> p (a b)")
            src = asb[:, :, :].rearrange("p a b -> p (a b)")
            own.done(dve.tensor_scalar(far[:, :], cnt, 0.0, FAR, ALU.is_equal, ALU.mult))
            own.mark(dve.memset(stat[:, 5:6], 0.0))
            own.done(dve.tensor_tensor_reduce(out=junk[:, :], in0=src, in1=far[:, :], scale=1.0, scalar=-3e38, op0=ALU.add, op1=ALU.max, accum_out=stat[:, 0:1]))
            own.done(dve.tensor_scalar(stat[:, 1:2], stat[:, 0:1], ad, None, ALU.add))
            own.mark(dve.scalar_tensor_tensor(stat[:, 2:3], stat[:, 1:2], NEG_SLOPE, stat[:, 1:2], ALU.mult, ALU.max))
            dve.wait_ge(L["line_ready"], d + 1)
            own.done(dve.scalar_tensor_tensor(prob[:, :], src, ad, prob[:, :], ALU.add, ALU.max))
            dve.tensor_scalar(prob[:, :], prob[:, :], stat[:, 2:3], 0.0, ALU.subtract, ALU.min).then_inc(L["arg_ready"], 1)
            if stats_of is not None:
                dve_row_stats(stats_of, own)
            dve.wait_ge(L["exp_ready"], d + 1)
            dve.scalar_tensor_tensor(prob[:, :], prob[:, :], 1.0, cnt, ALU.mult, ALU.mult, accum_out=stat[:, 3:4]).then_inc(L["probs_ready"], 1)
            dve.wait_ge(L["probs_ready"], d + 1)
            own.done(dve.reciprocal(rden[:, bass.ds(d, 1)], stat[:, 3:4]))
        PROB_STEPS = 7

        def dve_probs_low(l, d):
            L, dve = LAYER[l], nc.vector
            dve.wait_ge(L["pt_hi"], d + 1)
            dve.tensor_tensor(PT[1][:, :, :], blocks(0, NT)[0:T, :, 0:T], PT[0][:, :, :].bitcast(F32), ALU.subtract).then_inc(L["pt_lo"], 1)

        def dve_rows_out(l, d):
            L, dve = LAYER[l], nc.vector
            if l == 1:
                dve.wait_ge(x_plus_ready, d + 1)
                if not isinstance(d, int) or d >= 1:
                    dve.wait_ge(x2_stored, d * 32)
                    dve.wait_ge(xn2_ready, d)
            other = bias_b if l == 0 else x_plus
            for h in range(2):
                part = slice(h * HALF, (h + 1) * HALF)
                dve.wait_ge(L["rows_done"], 2 * d + 1 + h)
                dve.scalar_tensor_tensor(rows[:, part], bank(3 + h, T, HALF), rden[:, bass.ds(d, 1)], other[:, part], ALU.mult, ALU.add).then_inc(L["rows_out"], 1)

        def dve_row_stats(d, own):
            dve = nc.vector
            dve.wait_ge(LAYER[1]["rows_out"], 2 * d + 2)
            for h in range(2):
                last = dve.bn_stats(bn2[:, h, :], rows[:, h * HALF:(h + 1) * HALF])
            own.done(last)
            own.mark(dve.memset(stat[:, 6:7], 0.0))
            own.done(dve.bn_aggr(mv2[:, :], bn2[:, :, :]))
            dve.tensor_scalar(ln2[:, 0:1], mv2[:, 0:1], -1.0, None, ALU.mult)
            dve.tensor_scalar(ln2[:, 1:2], mv2[:, 1:2], LN_EPS, None, ALU.add).then_inc(var_ready, 1)
        STAT_STEPS = 3

        def dve_rows_low(l, d):
            L, dve = LAYER[l], nc.vector
            dve.wait_ge(L["xt_hi"], d + 1)
            src = blocks(row_bank(l, d), KC)[:, :, 0:T]
            if l == 0:
                dve.scalar_tensor_tensor(XT[1][:, :, :], src, 0.0, XT[0][:, :, :].bitcast(F32), ALU.max, ALU.subtract).then_inc(L["xt_lo"], 1)
            else:
                at = bass.ds(d * T, T)
                dve.tensor_tensor(xnT[1][:, :, at], src, xnT[0][:, :, at].bitcast(F32), ALU.subtract).then_inc(L["xt_lo"], 1)

        def dve_attention(l, own):
            L, dve = LAYER[l], nc.vector
            if l == 0:
                dve.memset(stat[:, 7:8], 0.0).then_inc(L["msgs_out"], 1)
                dve.wait_ge(h_free, NT + 1)
            else:
                dve.wait_ge(LAYER[0]["msgs_out"], NT + 1)
            own.done(dve.tensor_scalar(ad_slope[:, :], asd[:, :, 1], NEG_SLOPE, None, ALU.mult))
            dve.tensor_tensor(diag[:, :, :], ident[0:T, 0:T].rearrange("p (o a) -> p o a", o=1).to_broadcast([T, NT, T]),
                              asd[:, :, 0:1].to_broadcast([T, NT, T]), ALU.mult).then_inc(L["diag_ready"], 1)
            dve.wait_ge(L["asb_ready"], 1)
            dve_probs(l, 0, own)
            dve_probs_low(l, 0)
            dve_probs(l, 1, own)
            dve.wait_ge(L["bias_in"], 16)
            if l == 0:
                dve_rows_out(l, 0)
                dve_probs_low(l, 1)
                dve_probs(l, 2, own)
                dve_rows_low(l, 0)
                with dve.Fori(1, NT - 2) as d:
                    kept = own.enter(d - 1, PROB_STEPS)
                    dve_rows_out(l, d)
                    dve_probs_low(l, d + 1)
                    dve_probs(l, d + 2, own)
                    dve_rows_low(l, d)
                    own.leave(kept, NT - 3)
                dve_rows_out(l, NT - 2)
                dve_probs_low(l, NT - 1)
                dve_rows_low(l, NT - 2)
                dve_rows_out(l, NT - 1)
                dve_rows_low(l, NT - 1)
            else:
                dve_rows_out(l, 0)
                dve_probs_low(l, 1)
                dve_probs(l, 2, own, stats_of=0)
                with dve.Fori(1, NT - 2) as d:
                    kept = own.enter(d - 1, PROB_STEPS + STAT_STEPS)
                    dve_rows_out(l, d)
                    dve_probs_low(l, d + 1)
                    dve_probs(l, d + 2, own, stats_of=d)
                    dve_rows_low(l, d - 1)
                    own.leave(kept, NT - 3)
                dve_rows_out(l, NT - 2)
                dve_probs_low(l, NT - 1)
                dve_row_stats(NT - 2, own)
                dve_rows_low(l, NT - 3)
                dve_rows_out(l, NT - 1)
                dve_row_stats(NT - 1, own)
                dve_rows_low(l, NT - 2)

        def row_bank(l, d):
            return 5 if l == 1 and not (isinstance(d, int) and d >= NT - 2) else 0

        def pe_attention(l):
            L, pe = LAYER[l], nc.tensor
            pe.wait_ge(L["diag_ready"], 1)
            for s in range(NT):
                last = pe.matmul(blocks(0, NT)[0:T, s, 0:T], ones[0:T, 0:T], diag[:, s, :], start=True, stop=True)
            last.then_inc(L["asb_turned"], 1)

            def turn_probs(d):
                pe.wait_ge(L["probs_ready"], d + 1)
                if isinstance(d, int) and d == 0:
                    pe.wait_ge(L["asb_ready"], 1)
                if l == 0 and (not isinstance(d, int) or d >= 2):
                    pe.wait_ge(L["xt_lo"], d - 1)
                for s in range(NT):
                    last = pe.transpose(blocks(0, NT)[0:T, s, 0:T], prob[:, s * T:(s + 1) * T], ident[0:T, 0:T])
                last.then_inc(L["probs_turned"], 1)

            def mix(d):
                pe.wait_ge(L["pt_hi"], d + 1)
                for h in range(2):
                    if not isinstance(d, int) or d >= 1:
                        pe.wait_ge(L["rows_out"], 2 * d - 1 + h)
                    for n in range(3 * NT):
                        if h == 0 and n == 2 * NT:
                            pe.wait_ge(L["pt_lo"], d + 1)
                        (a, b), s = HIGH_FIRST[n // NT], n % NT
                        last = pe.matmul(bank(3 + h, T, HALF), PT[a][:, s, :], H[b][:, s, h * HALF:(h + 1) * HALF], start=(n == 0), stop=(n == 3 * NT - 1))
                    last.then_inc(L["rows_done"], 1)

            def turn_out(d, n):
                src = rows if l == 0 else xn2
                if l == 0:
                    pe.wait_ge(L["rows_out"], 2 * d + 2)
                    pe.wait_ge(L["pt_lo"], n)
                else:
                    pe.wait_ge(xn2_ready, d + 1)
                    if not isinstance(d, int) or d >= 1:
                        pe.wait_ge(L["xt_lo"], d)
                for k in range(KC):
                    last = pe.transpose(blocks(row_bank(l, d), KC)[:, k, 0:T], src[:, k * P:(k + 1) * P], ident[0:T, 0:T])
                last.then_inc(L["rows_turned"], 1)

            def next_messages(d):
                if l == 1:
                    return
                pe.wait_ge(L["xt_lo"], d + 1)
                pe.wait_ge(L["msgs_out"], d + 1)
                for h, (lo, hi) in enumerate(((0, HALF), (HALF, WX))):
                    for n in range(3 * KC):
                        (a, b), k = PARTS[n // KC], n % KC
                        last = pe.matmul(bank(5 + h, T, hi - lo), XT[a][:, k, :], Wg[b][:, k, lo:hi], start=(n == 0), stop=(n == 3 * KC - 1))
                last.then_inc(L["msgs_done"], 1)

            turn_probs(0)
            if l == 1:
                pe.wait_ge(split_dve, NT // 2)
                pe.wait_ge(split_pool, NT // 2)
            mix(0)
            turn_probs(1)
            if l == 0:
                turn_out(0, 2)
                pe.wait_ge(w2_lo, 1)
                with pe.Fori(1, NT - 1) as d:
                    mix(d)
                    turn_probs(d + 1)
                    next_messages(d - 1)
                    turn_out(d, d + 2)
                mix(NT - 1)
                next_messages(NT - 2)
                turn_out(NT - 1, NT)
                next_messages(NT - 1)
            else:
                mix(1)
                turn_probs(2)
                turn_out(0, 0)
                with pe.Fori(2, NT - 1) as d:
                    mix(d)
                    turn_probs(d + 1)
                    turn_out(d - 1, 0)
                mix(NT - 1)
                turn_out(NT - 2, 0)
                pe_columns("q", 0, range(0, HC))
                turn_out(NT - 1, 0)

        order = []
        for e in range(HEADS):
            if e == 0:
                order += [("q", e, n) for n in range(HC * 3)]
            order += [("k", e, n) for n in range(HC * 3)] + [("v", e, 0)]
            for i in range(NT):
                if i + 1 < NT:
                    order.append(("v", e, i + 1))
                elif e + 1 < HEADS:
                    order += [("q", e + 1, n) for n in range(HC * 3)]
                order.append(("y", e, i))
        USE = {key: n for n, key in enumerate(order)}
        HIGH = {key: n for n, key in enumerate(k for k in order if k[0] != "y" and k[:2] != ("q", 0))}

        def column_group(n):
            c, (start, size) = n % HC, SPAN[n // HC]
            return c, start, size

        def bias_col(kind, e, c):
            col = (KC if kind == "k" else 0) + e * HC + c
            return bqk_c[:, col:col + 1]

        def seen(i):
            return (i + 1) * T

        def pe_group(key):
            u = USE[key]
            if u >= 2:
                nc.tensor.wait_ge(group_free, u - 1)
            return 6 + u % 2

        def pe_columns(kind, e, groups=range(HC * 3)):
            slot = "qk".index(kind)
            nc.tensor.wait_ge(ws_lo, 3 * e + slot + 1)
            for n in groups:
                b = pe_group((kind, e, n))
                c, start, size = column_group(n)
                for m in range(3 * KC):
                    (x_, y_), k = PARTS[m // KC], m % KC
                    last = nc.tensor.matmul(bank(b, P, size), Ws[x_][slot][:, k, c * P:(c + 1) * P], xnT[y_][:, k, start:start + size],
                                            start=(m == 0), stop=(m == 3 * KC - 1))
                last.then_inc(group_done, 1)

        def pe_values(e, i):
            width = WG if e == 0 else HD
            nc.tensor.wait_ge(ws_lo, 3 * e + 3)
            b = pe_group(("v", e, i))
            for m in range(3 * KC):
                (x_, y_), k = PARTS[m // KC], m % KC
                last = nc.tensor.matmul(bank(b, T, width), xnT[x_][:, k, i * T:(i + 1) * T], Ws[y_][2][:, k, 0:width], start=(m == 0), stop=(m == 3 * KC - 1))
            last.then_inc(group_done, 1)

        def pe_scores(e, i):
            if i == 0:
                nc.tensor.wait_ge(group_free, USE["k", e, HC * 3 - 1] + 1)
            if e or i:
                nc.tensor.wait_ge(pexp_ready, e * NT + i)
            width = seen(i) + seen(i) % 2
            for j in range(0, width, BANK):
                size = min(BANK, width - j)
                for m in range(3 * HC):
                    (x_, y_), c = PARTS[m // HC], m % HC
                    last = nc.tensor.matmul(bank(j // BANK, T, size), qT[x_][:, c, i * T:(i + 1) * T], kT[y_][:, c, j:j + size], start=(m == 0), stop=(m == 3 * HC - 1))
            last.then_inc(scores_done, 1)

        def pe_turn(e, i):
            t = e * NT + i
            nc.tensor.wait_ge(pexp_ready, t + 1)
            if t:
                nc.tensor.wait_ge(pexp_lo, t)
            for s in range(i + 1):
                last = nc.tensor.transpose(blocks(3, NT)[0:T, s, 0:T], pexp[0:T, s * T:(s + 1) * T], ident[0:T, 0:T])
            last.then_inc(pexp_turned, 1)

        def pe_weighted(e, i):
            b = pe_group(("y", e, i))
            nc.tensor.wait_ge(pexp_lo, e * NT + i + 1)
            nc.tensor.wait_ge(group_free, USE["v", e, i] + 1)
            for m in range(3 * (i + 1)):
                (x_, y_), s = PARTS[m // (i + 1)], m % (i + 1)
                last = nc.tensor.matmul(bank(b, T, HD), pT[x_][:, s, :], vs[y_][:, s, :], start=(m == 0), stop=(m == 3 * (i + 1) - 1))
            last.then_inc(group_done, 1)

        def pe_ffn(pe):
            pe_columns("q", 0, range(HC, 2 * HC))
            pe.wait_ge(LAYER[1]["xt_lo"], NT)
            pe_columns("q", 0, range(2 * HC, 3 * HC))
            for e in range(HEADS):
                pe_columns("k", e)
                pe_scores(e, 0)
                pe_values(e, 0)
                for i in range(NT):
                    pe_turn(e, i)
                    if i + 1 < NT:
                        pe_scores(e, i + 1)
                        pe_values(e, i + 1)
                    elif e + 1 < HEADS:
                        pe_columns("q", e + 1)
                    pe_weighted(e, i)

        def act_weight(b):
            width = WG if b == 2 else WB
            nc.scalar.wait_ge(ws_in, 16 * (b + 1 + (b >= 2)))
            if b >= 3:
                e, kind = (b - 3) // 3, "qkv"[b % 3]
                nc.scalar.wait_ge(group_done, USE[kind, e, (NT if kind == "v" else HC * 3) - 1] + 1)
            nc.scalar.activation(Ws[0][b % 3][:, :, 0:width], w_raw[:, :, 0:width], ACT.Copy).then_inc(ws_hi, 1)

        def act_columns(kind, e):
            to = (qT if kind == "q" else kT)[0]
            for n in range(HC * 3):
                c, start, size = column_group(n)
                u = USE[kind, e, n]
                nc.scalar.wait_ge(group_done, u + 1)
                nc.scalar.activation(to[:, c, start:start + size], bank(6 + u % 2, P, size), ACT.Identity, bias=bias_col(kind, e, c)).then_inc(group_hi, 1)

        def act_values(e, i):
            u = USE["v", e, i]
            nc.scalar.wait_ge(group_done, u + 1)
            nc.scalar.activation(vs[0][:, i, :], bank(6 + u % 2, T, HD), ACT.Copy).then_inc(group_hi, 1)

        def act_exp(e, i):
            nc.scalar.wait_ge(max_ready, e * NT + i + 1)
            r = i % 2
            nc.scalar.activation(pexp[0:T, 0:seen(i)], PS[0:T, 0:3, :].rearrange("p b c -> p (b c)")[:, 0:seen(i)], ACT.Exp,
                                 bias=att_max[:, 2 + r:3 + r], scale=SCALE, accum_out=att_den[:, r:r + 1]).then_inc(pexp_ready, 1)

        def act_turned(e, i):
            nc.scalar.wait_ge(pexp_turned, e * NT + i + 1)
            nc.scalar.activation(pT[0][:, 0:i + 1, :], blocks(3, NT)[0:T, 0:i + 1, 0:T], ACT.Copy).then_inc(pexp_hi, 1)

        def act_ffn(act):
            act_rows_high(1, NT - 1)
            for b in range(1, 3):
                act_weight(b)
            act.wait_ge(tabs_in, TABS)
            for c in range(HC):
                act.wait_ge(conv_ready, c + 1)
                act.activation(qT[0][:, c, :], pexp[:, :], ACT.Copy).then_inc(conv_hi, 1)
            for e in range(HEADS):
                act_columns("k", e)
                act_exp(e, 0)
                act_values(e, 0)
                for i in range(NT):
                    act_turned(e, i)
                    if i + 1 < NT:
                        act_exp(e, i + 1)
                        act_values(e, i + 1)
                    elif e + 1 < HEADS:
                        act_columns("q", e + 1)
                    if i in (2, 5, NT - 2):
                        act_weight(3 * e + 3 + (2, 5, NT - 2).index(i))
                    if e == 0 and i == NT - 1:
                        act.wait_ge(gate_arg, 1)
                        act.activation(gate_e[:, :, :], gate_e[:, :, :], ACT.Exp).then_inc(gate_exp, 1)
                        act.wait_ge(gate_arg, 2)
                        act.activation(gate_e[:, :, :], gate_e[:, :, :], ACT.Exp).then_inc(gate_exp, 1)

        def dve_columns(kind, e):
            to = qT if kind == "q" else kT
            for n in range(HC * 3):
                c, start, size = column_group(n)
                u = USE[kind, e, n]
                nc.vector.wait_ge(group_hi, HIGH[kind, e, n] + 1)
                nc.vector.scalar_tensor_tensor(to[1][:, c, start:start + size], bank(6 + u % 2, P, size), bias_col(kind, e, c),
                                               to[0][:, c, start:start + size].bitcast(F32), ALU.add, ALU.subtract).then_inc(group_free, 1)

        def dve_first_queries(own):
            dve = nc.vector
            own.mark(dve.memset(q_raw[:, :, 0:1], 0.0))
            own.mark(dve.memset(q_raw[:, :, N + 1:N + 2], 0.0))

            def queries(groups):
                for n in groups:
                    c, start, size = column_group(n)
                    u = USE["q", 0, n]
                    dve.wait_ge(group_done, u + 1)
                    dve.tensor_scalar(q_raw[:, c, 1 + start:1 + start + size], bank(6 + u % 2, P, size), bias_col("q", 0, c), None, ALU.add).then_inc(group_free, 1)

            queries(range(0, HC))
            dve_rows_low(1, NT - 1)
            queries(range(HC, 3 * HC))
            own.wait()
            dve.wait_ge(group_free, 3 * HC)
            for c in range(HC):
                own.done(dve.tensor_scalar(pexp[:, :], q_raw[:, c, 1:N + 1], conv_wc[:, c, 1:2], conv_bc[:, c:c + 1], ALU.mult, ALU.add))
                own.done(dve.scalar_tensor_tensor(pexp[:, :], q_raw[:, c, 0:N], conv_wc[:, c, 0:1], pexp[:, :], ALU.mult, ALU.add))
                dve.scalar_tensor_tensor(pexp[:, :], q_raw[:, c, 2:N + 2], conv_wc[:, c, 2:3], pexp[:, :], ALU.mult, ALU.add).then_inc(conv_ready, 1)
                dve.wait_ge(conv_hi, c + 1)
                own.done(dve.tensor_tensor(qT[1][:, c, :], pexp[:, :], qT[0][:, c, :].bitcast(F32), ALU.subtract))

        def dve_values(e, i):
            u = USE["v", e, i]
            nc.vector.wait_ge(group_hi, HIGH["v", e, i] + 1)
            if e == 0:
                nc.vector.tensor_tensor(gate_h[:, i, :], PS[0:T, 6 + u % 2, HD:WG], bg1_b[:, :], ALU.add)
            nc.vector.tensor_tensor(vs[1][:, i, :], bank(6 + u % 2, T, HD), vs[0][:, i, :].bitcast(F32), ALU.subtract).then_inc(group_free, 1)

        def dve_max(e, i, own):
            dve, r = nc.vector, i % 2
            s = PS[0:T, 0:3, :].rearrange("p b c -> p (b c)")
            dve.wait_ge(scores_done, e * NT + i + 1)
            own.done(dve.tensor_tensor(s[:, i * T:seen(i)], s[:, i * T:seen(i)], tri[:, :], ALU.add))
            own.done(dve.tensor_reduce(att_max[:, r:r + 1], s[:, 0:seen(i)], AX.X, ALU.max))
            dve.tensor_scalar(att_max[:, 2 + r:3 + r], att_max[:, r:r + 1], -SCALE, None, ALU.mult).then_inc(max_ready, 1)

        def dve_turned(e, i):
            nc.vector.wait_ge(pexp_hi, e * NT + i + 1)
            nc.vector.tensor_tensor(pT[1][:, 0:i + 1, :], blocks(3, NT)[0:T, 0:i + 1, 0:T], pT[0][:, 0:i + 1, :].bitcast(F32), ALU.subtract).then_inc(pexp_lo, 1)

        def dve_weighted(e, i, own):
            dve, r, u, m = nc.vector, i % 2, USE["y", e, i], e * NT + i
            own.done(dve.reciprocal(att_den[:, 2 + r:3 + r], att_den[:, r:r + 1]))
            dve.wait_ge(group_done, u + 1)
            if m >= 2:
                dve.wait_ge(ys_stored[m % 2], 32 * (m // 2))
            dve.scalar_tensor_tensor(ys_out[:, m % 2, :], bank(6 + u % 2, T, HD), att_den[:, 2 + r:3 + r],
                                     bv_b[:, e * HD:(e + 1) * HD], ALU.mult, ALU.add).then_inc(group_free, 1)

        def dve_gate(own):
            dve = nc.vector
            flat = gate_h[:, :, :].rearrange("p a b -> p (a b)")
            own.done(dve.tensor_scalar(flat, flat, 0.0, None, ALU.max))
            for e in range(HEADS):
                own.done(dve.tensor_tensor(gate_t[:, :, :], gate_h[:, :, :], wg2_b[:, :, e:e + 1].rearrange("p a b -> p b a").to_broadcast([T, NT, GATE]), ALU.mult))
                own.done(dve.tensor_reduce(gate_e[:, e, :], gate_t[:, :, :], AX.X, ALU.add))
                own.done(dve.tensor_scalar(gate_e[:, e, :], gate_e[:, e, :], bg2_b[:, e:e + 1], None, ALU.add))

            def less_max():
                own.done(dve.tensor_tensor(gate_c[:, 0, :], gate_e[:, 0, :], gate_e[:, 1, :], ALU.max))
                own.done(dve.tensor_tensor(gate_c[:, 0, :], gate_c[:, 0, :], gate_e[:, 2, :], ALU.max))
                dve.tensor_tensor(gate_e[:, :, :], gate_e[:, :, :], gate_c[:, 0:1, :].to_broadcast([T, HEADS, NT]), ALU.subtract).then_inc(gate_arg, 1)

            def over_sum(to, frm):
                own.done(dve.tensor_tensor(gate_c[:, 0, :], frm[:, 0, :], frm[:, 1, :], ALU.add))
                own.done(dve.tensor_tensor(gate_c[:, 0, :], gate_c[:, 0, :], frm[:, 2, :], ALU.add))
                own.done(dve.reciprocal(gate_c[:, 0, :], gate_c[:, 0, :]))
                return dve.tensor_tensor(to[:, :, :], frm[:, :, :], gate_c[:, 0:1, :].to_broadcast([T, HEADS, NT]), ALU.mult)

            less_max()
            dve.wait_ge(gate_exp, 1)
            own.done(over_sum(gate_e, gate_e))
            g = [gate_e[:, e, :] for e in range(HEADS)]
            tests = (((0, 1, ALU.is_lt), (0, 2, ALU.is_lt)), ((1, 0, ALU.is_le), (1, 2, ALU.is_lt)), ((2, 0, ALU.is_le), (2, 1, ALU.is_le)))
            for e, pair in enumerate(tests):
                for n, (a_, b_, op) in enumerate(pair):
                    own.mark(dve.tensor_tensor(gate_c[:, 1 + n, :], g[a_], g[b_], op))
                own.wait()
                own.done(dve.tensor_tensor(gate_c[:, 3, :], gate_c[:, 1, :], gate_c[:, 2, :], ALU.mult))
                own.done(dve.tensor_scalar(gate_scale[:, e, :], gate_c[:, 3, :], -1.0, 1.0, ALU.mult, ALU.add))
            less_max()
            dve.wait_ge(gate_exp, 2)
            own.done(dve.tensor_tensor(gate_e[:, :, :], gate_e[:, :, :], gate_scale[:, :, :], ALU.mult))
            over_sum(gate_scale, gate_e).then_inc(gate_ready, 1)

        def dve_ffn(dve, own):
            dve.wait_ge(tabs_in, TABS)
            dve_first_queries(own)
            dve.wait_ge(tri_ready, 2)
            for e in range(HEADS):
                dve_columns("k", e)
                dve_max(e, 0, own)
                dve_values(e, 0)
                for i in range(NT):
                    dve_turned(e, i)
                    if i + 1 < NT:
                        dve_max(e, i + 1, own)
                        dve_values(e, i + 1)
                    elif e + 1 < HEADS:
                        dve_columns("q", e + 1)
                    dve_weighted(e, i, own)
                if e == 0:
                    dve_gate(own)

        def pool_ffn(pool):
            pool.wait_ge(LAYER[1]["probs_ready"], NT)
            pool.memset(tri[:, :], 0.0).then_inc(tri_ready, 1)
            pool.wait_ge(tri_ready, 1)
            pool.affine_select(out=tri[:, :], in_=tri[:, :], compare_op=ALU.is_ge, fill=FAR,
                               base=0, pattern=[[-1, T]], channel_multiplier=1).then_inc(tri_ready, 1)
            for b in range(1, BLOCKS + HEADS):
                pool_weight(pool, b)

        def pool_weight(pool, b):
            width = WG if b == 2 else WB
            pool.wait_ge(ws_hi, b + 1)
            pool.tensor_tensor(Ws[1][b % 3][:, :, 0:width], w_raw[:, :, 0:width], Ws[0][b % 3][:, :, 0:width].bitcast(F32), ALU.subtract).then_inc(ws_lo, 1)

        TABS = 16 * 7

        def sp_ffn(sp):
            L = LAYER[1]
            sp.wait_ge(L["probs_ready"], NT)
            with nc.allow_non_contiguous_dma(reason="small tables, a column for each chunk"):
                sp.dma_start(bqk_c[:, :], ffn["bqk"].rearrange("(c p) -> p c", p=P)).then_inc(tabs_in, 16)
                sp.dma_start(conv_wc[:, :, :], ffn["conv_w"].rearrange("(c p) o k -> p c (o k)", p=P)).then_inc(tabs_in, 16)
                sp.dma_start(conv_bc[:, :], ffn["conv_b"].rearrange("(c p) -> p c", p=P)).then_inc(tabs_in, 16)
            for to, frm in ((bg1_b, ffn["bg1"]), (bg2_b, ffn["bg2"])):
                sp.dma_start(to[:, :], frm.rearrange("(o n) -> o n", o=1).to_broadcast([T, frm.shape[0]])).then_inc(tabs_in, 16)
            sp.dma_start(wg2_b[:, :, :].rearrange("p a b -> p (a b)"), ffn["Wg2"].rearrange("(o a) b -> o (a b)", o=1).to_broadcast([T, GATE * HEADS])).then_inc(tabs_in, 16)
            sp.dma_start(bv_b[:, :], ffn["bv"].rearrange("(o a) b -> o (a b)", o=1).to_broadcast([T, D])).then_inc(tabs_in, 16)

        @block.sync
        def _(sp):
            sp.dma_start(dst_i[:, :], dst.rearrange("(g e) -> g e", g=G)).then_inc(edges_in, 16)
            sp.dma_start(src_i[:, :], src.rearrange("(g e) -> g e", g=G)).then_inc(edges_in, 16)
            with nc.allow_non_contiguous_dma(reason="the first destination of each group"):
                sp.dma_start(bases[:, :], dst.rearrange("(o g e) -> o g e", g=G, o=1)[:, :, 0]).then_inc(bases_in, 16)
            for c in range(KC):
                sp.dma_start(Wraw[:, c, 0:D], gnn[0]["W"][c * P:(c + 1) * P, :]).then_inc(w_in, 16)
            xr = x.rearrange("(t p) d -> p t d", p=T)
            rows_in(sp, xall[:, 0:5, :], xr[:, 0:5, :], x_in)
            rows_in(sp, xall[:, 5:NT, :], xr[:, 5:NT, :], x_in)
            sp.wait_ge(xn_ready, NT)
            for c in range(KC):
                sp.dma_start(Wraw2[:, c, 0:D], gnn[1]["W"][c * P:(c + 1) * P, :]).then_inc(w2_in, 16)
            for a, name in enumerate(("as", "ad")):
                sp.dma_start(attb2[:, a, :], gnn[1][name].rearrange("(o n) -> o n", o=1).to_broadcast([P, D])).then_inc(att2_in, 16)
            sp.wait_ge(counts_ready, NT)
            sp.dma_start(bias_b[:, :], gnn[0]["b"].rearrange("(o n) -> o n", o=1).to_broadcast([T, D])).then_inc(LAYER[0]["bias_in"], 16)
            sp.wait_ge(LAYER[0]["rows_out"], 2 * NT)
            sp.dma_start(bias_b[:, :], gnn[1]["b"].rearrange("(o n) -> o n", o=1).to_broadcast([T, D])).then_inc(LAYER[1]["bias_in"], 16)
            sp.wait_ge(split_hi, NT)
            sp.wait_ge(split_dve, NT // 2)
            sp.wait_ge(split_pool, NT // 2)
            x2r = x2_dram.rearrange("(t p) d -> t p d", p=T)
            xt = x.rearrange("(t p) d -> t p d", p=T)
            def weight_in(b):
                if b:
                    sp.wait_ge(ws_lo, b)
                if b < BLOCKS and b % 3 < 2:
                    col = (b % 3) * D + (b // 3) * HD
                    frm = ffn["Wqk"][:, col:col + WB]
                elif b < BLOCKS:
                    frm = ffn["Wv"][b // 3]
                else:
                    frm = ffn["Wp"][:, (b - BLOCKS) * WB:(b - BLOCKS + 1) * WB]
                sp.dma_start(w_raw[:, :, 0:WB], frm.rearrange("(k p) n -> p k n", p=P)).then_inc(ws_in, 16)
                if b == 2:
                    sp.dma_start(w_raw[:, :, WB:WG], ffn["Wg1"].rearrange("(k p) n -> p k n", p=P)).then_inc(ws_in, 16)

            rows_in(sp, x_plus, xt[0], x_again)
            weight_in(0)
            for d in range(NT):
                sp.wait_ge(LAYER[1]["rows_out"], 2 * d + 2)
                rows_out_to(sp, x2r[d], rows, x2_stored)
                if d + 1 < NT:
                    rows_in(sp, x_plus, xt[d + 1], x_again)
                if d == NT - 2:
                    sp_ffn(sp)
            sp.wait_ge(x2_stored, 32 * NT)
            for b in range(1, 4):
                weight_in(b)
            yr = y_dram.rearrange("(t p) d -> t p d", p=T)
            for m in range(HEADS * NT):
                e, i = m // NT, m % NT
                sp.wait_ge(group_free, USE["y", e, i] + 1)
                rows_out_to(sp, yr[i][:, e * HD:(e + 1) * HD], ys_out[:, m % 2, :], ys_stored[m % 2])
                if i in (2, 5, NT - 2) and m < HEADS * NT - 2:
                    weight_in(3 * e + 4 + (2, 5, NT - 2).index(i))
            x2r = x2_dram.rearrange("(t p) d -> t p d", p=T)
            outr = out.rearrange("(t p) d -> t p d", p=T)
            for p in range(2):
                sp.wait_ge(ys_stored[p], 32 * HEADS * NT // 2)
            sp.dma_start(bp_b[:, :], ffn["bp"].rearrange("(o n) -> o n", o=1).to_broadcast([T, D])).then_inc(bp_in, 16)
            for i in range(2):
                rows_in(sp, y_in[:, i, :], yr[i], y_loaded[i])
                rows_in(sp, x2_in[:, i, :], x2r[i], x2_loaded[i])
            for i in range(NT):
                if i + 2 < NT:
                    sp.wait_ge(y_turned, i + 1)
                    rows_in(sp, y_in[:, i % 2, :], yr[i + 2], y_loaded[i % 2])
                sp.wait_ge(out_ready, i + 1)
                rows_out_to(sp, outr[i], out_sb[:, i % 2, :], out_stored[i % 2])
                if i + 2 < NT:
                    rows_in(sp, x2_in[:, i % 2, :], x2r[i + 2], x2_loaded[i % 2])
            for p in range(2):
                sp.wait_ge(out_stored[p], 32 * NT // 2)


        def rows_split(pool, i, n):
            pool.wait_ge(xt_hi_ready, n)
            pool.wait_ge(xt_raw_ready, n)
            pool.tensor_tensor(XT[1][:, :, :], xt_raw[:, :, :], XT[0][:, :, :].bitcast(F32), ALU.subtract).then_inc(xt_lo_ready, 1)
            pool.wait_ge(h_hi_ready, n)
            pool.tensor_tensor(H[1][:, bass.ds(i, 1), :].rearrange("p a d -> p (a d)"), h_raw[:, 0:D],
                               H[0][:, bass.ds(i, 1), :].rearrange("p a d -> p (a d)").bitcast(F32), ALU.subtract).then_inc(h_lo_ready, 1)

        @block.gpsimd
        def _(pool):
            own = Own(pool, pool_own)
            own.mark(pool.memset(ident[:, :], 0.0))
            pool.memset(ones[:, :], 1.0).then_inc(consts_ready, 1)
            pool.memset(minus_half[:, :], -0.5).then_inc(h_free, 1)
            own.done(pool.iota(iota_i[:, :], pattern=[[1, NT * W]], base=0, channel_multiplier=0))
            pool.tensor_copy(iota[:, :], iota_i[:, :]).then_inc(consts_ready, 1)
            pool.affine_select(out=ident[:, :], in_=ident[:, :], compare_op=ALU.not_equal, fill=1.0,
                               base=0, pattern=[[-1, P]], channel_multiplier=1).then_inc(consts_ready, 1)
            pool.memset(countsT[:, :, :].rearrange("p a b -> p (a b)").bitcast(mybir.dt.uint32), 0).then_inc(countsT_zero, 1)
            pool.wait_ge(consts_ready, 3)
            pool.wait_ge(stats_ready, 1)
            own.done(pool.tensor_tensor(rstd[:, :], varep[:, :], minus_half[:, :], ALU.pow))
            pool.tensor_tensor(shift[:, :], negmean[:, :], rstd[:, :], ALU.mult).then_inc(scale_ready, 1)
            pool.wait_ge(w_hi_ready, 1)
            pool.tensor_tensor(Wg[1][:, :, :], Wraw[:, :, :], Wg[0][:, :, :].bitcast(F32), ALU.subtract).then_inc(w_lo_ready, 1)
            with pool.Fori(0, NT - 1) as i:
                rows_split(pool, i, i + 1)
            rows_split(pool, NT - 1, NT)
            pool.wait_ge(w2_hi, 1)
            pool.tensor_tensor(Wg[1][:, :, :], Wraw2[:, :, :], Wg[0][:, :, :].bitcast(F32), ALU.subtract).then_inc(w2_lo, 1)
            for s in range(1, NT, 2):
                pool.wait_ge(split_hi, s + 1)
                pool.tensor_tensor(H[1][:, s, :], h_next[:, s, :], H[0][:, s, :].bitcast(F32), ALU.subtract).then_inc(split_pool, 1)
            L = LAYER[1]
            pool.wait_ge(split_dve, NT // 2)
            pool.wait_ge(split_pool, NT // 2)
            pool.memset(half2[:, :], -0.5).then_inc(half_ready, 1)
            pool.wait_ge(L["bias_in"], 16)
            pool.wait_ge(half_ready, 1)
            for d in range(NT):
                pool.wait_ge(x_again, 32 * (d + 1))
                pool.tensor_tensor(x_plus[:, :], x_plus[:, :], bias_b[:, :], ALU.add).then_inc(x_plus_ready, 1)
                pool.wait_ge(var_ready, d + 1)
                own.done(pool.tensor_tensor(ln2[:, 2:3], ln2[:, 1:2], half2[:, :], ALU.pow))
                pool.tensor_tensor(ln2[:, 3:4], ln2[:, 0:1], ln2[:, 2:3], ALU.mult).then_inc(ln_ready, 1)
                if d == 0:
                    pool_weight(pool, 0)
            pool_ffn(pool)
            pool.wait_ge(bp_in, 16)
            for i in range(NT):
                pool.wait_ge(x2_loaded[i % 2], 32 * (i // 2 + 1))
                pool.tensor_tensor(x2_in[:, i % 2, :], x2_in[:, i % 2, :], bp_b[:, :], ALU.add).then_inc(x2_plus, 1)

        def normalise(i):
            nc.scalar.activation(xn[:, :], xall[:, bass.ds(i, 1), :].rearrange("p a d -> p (a d)"), ACT.Identity,
                                 bias=shift[:, bass.ds(i, 1)], scale=rstd[:, bass.ds(i, 1)]).then_inc(xn_ready, 1)

        def act_rows(i, n):
            nc.scalar.wait_ge(xn_turned, n)
            nc.scalar.activation(xt_raw[:, :, :], blocks(0, KC)[:, :, 0:T], ACT.Copy).then_inc(xt_raw_ready, 1)
            nc.scalar.activation(XT[0][:, :, :], blocks(0, KC)[:, :, 0:T], ACT.Copy).then_inc(xt_hi_ready, 1)

        def act_messages(i, n):
            nc.scalar.wait_ge(h_done, n)
            nc.scalar.activation(h_raw[:, 0:HALF], bank(5, T, HALF), ACT.Copy)
            nc.scalar.activation(h_raw[:, HALF:WX], bank(6, T, WX - HALF), ACT.Copy)
            hi = H[0][:, bass.ds(i, 1), :].rearrange("p a d -> p (a d)")
            nc.scalar.activation(hi[:, 0:HALF], bank(5, T, HALF), ACT.Copy)
            nc.scalar.activation(hi[:, HALF:D], bank(6, T, HALF), ACT.Copy).then_inc(h_hi_ready, 1)
            nc.scalar.activation(asd[:, bass.ds(i, 1), :].rearrange("p a b -> p (a b)"), PS[0:T, 6, HALF:HALF + 2], ACT.Copy).then_inc(h_free, 1)

        @block.scalar
        def _(act):
            act.dma_start(attb[:, 0, :], gnn[0]["as"].rearrange("(o n) -> o n", o=1).to_broadcast([P, D])).then_inc(att_in, 16)
            act.dma_start(attb[:, 1, :], gnn[0]["ad"].rearrange("(o n) -> o n", o=1).to_broadcast([P, D])).then_inc(att_in, 16)
            act.wait_ge(edge_rows_turned, 1)
            for b, t in ((0, tab_low), (1, tab_win)):
                for c in range(2):
                    act.activation(t[:, :, :, c].rearrange("p g t -> p t g"), bank(b, T, ET * G).rearrange("p (t g) -> p t g", t=ET), ACT.Copy)
            for b, t in ((2, tab_dst), (3, tab_high)):
                act.activation(t[:, :, :].rearrange("p a b -> p (a b)"), bank(b, T, ET * G), ACT.Copy)
            act.activation(flag[:, :], bank(4, 1, 1), ACT.Copy).then_inc(tables_ready, 1)
            act.wait_ge(w_in, 16 * KC)
            act.wait_ge(att_cols_ready, 1)
            act.activation(Wg[0][:, :, :], Wraw[:, :, :], ACT.Copy).then_inc(w_hi_ready, 1)
            act.wait_ge(scale_ready, 1)
            normalise(0)
            with act.Fori(0, NT - 1) as i:
                act_rows(i, i + 1)
                normalise(i + 1)
                act_messages(i, i + 1)
            act_rows(NT - 1, NT)
            act_messages(NT - 1, NT)
            act.wait_ge(countsT_ready, 1)
            for d in range(NT):
                if d >= 2:
                    act.wait_ge(ct_turned, d - 1)
                act.activation(ct_f[:, d % 2, :, :], countsT[:, :, d * T:(d + 1) * T], ACT.Copy).then_inc(ct_conv, 1)

            act_attention(0)
            act.wait_ge(LAYER[0]["rows_done"], 2 * NT)
            for s in range(NT):
                act.wait_ge(LAYER[0]["msgs_out"], s + 2)
                act.activation(H[0][:, s, :], h_next[:, s, :], ACT.Copy).then_inc(split_hi, 1)
            act_attention(1)
            act_ffn(act)

            def scale(i):
                act.wait_ge(y_loaded[i % 2], 32 * (i // 2 + 1))
                for e in range(HEADS):
                    part = y_in[:, i % 2, e * HD:(e + 1) * HD]
                    last = act.activation(part, part, ACT.Copy, scale=gate_scale[:, e, i:i + 1])
                last.then_inc(y_scaled, 1)

            act.wait_ge(gate_ready, 1)
            scale(0)
            for i in range(NT):
                if i + 1 < NT:
                    scale(i + 1)
                act.wait_ge(y_turned, i + 1)
                if i >= 2:
                    act.wait_ge(proj_done, i - 1)
                act.activation(yT[0][:, i % 2, :, :], blocks(2 * (i % 2), KC)[:, :, 0:T], ACT.Copy).then_inc(yt_hi, 1)

        def onehots(g, buf):
            for hot, n, tab in ((oh_src, OHS, tab_low), (oh_win, NT * W, tab_win)):
                last = nc.vector.tensor_tensor(hot[:, buf, :, :].rearrange("p t (n c) -> p t n c", c=2),
                                               iota[:, 0:n].rearrange("p (o n c) -> p o n c", o=1, c=2).to_broadcast([T, ET, n // 2, 2]),
                                               tab[:, bass.ds(g, 1), :, :].rearrange("p g t (o c) -> p (g t) o c", o=1).to_broadcast([T, ET, n // 2, 2]), ALU.is_equal)
            last.then_inc(onehots_ready, 1)

        def add_window(dve, q, buf, start):
            dve.wait_ge(group_counted, q + 1)
            cols = countsT[:, :, bass.ds(start, W)]
            nc.vector.tensor_tensor(cols, bank(3 + buf % 2, T, NT * W).rearrange("p (a b) -> p a b", a=NT), cols, ALU.add).then_inc(window_free, 1)

        def put_counts(dve, d):
            dve.wait_ge(ct_turned, d + 1)
            nc.vector.tensor_copy(counts[:, d, :].rearrange("p (a b) -> p a b", a=NT), blocks(3 * (d % 2), NT)[0:T, :, 0:T]).then_inc(counts_ready, 1)

        @block.vector
        def _(dve):
            own = Own(dve, dve_own)
            nc.vector.memset(small[:, 0:1], 0.0).then_inc(window_free, 2)
            dve.wait_ge(edges_in, 32)
            own.mark(nc.vector.tensor_copy(dst_f[:, :], dst_i[:, :]))
            own.done(nc.vector.tensor_scalar(src_high[:, :], src_i[:, :], -(T - 1) / 2, 1.0 / T, ALU.add, ALU.mult))
            own.done(nc.vector.tensor_scalar(src_high[:, :], src_high[:, :], ROUND, ROUND, ALU.add, ALU.subtract))
            own.mark(nc.vector.scalar_tensor_tensor(src_low[:, :], src_high[:, :], -float(T), src_i[:, :], ALU.mult, ALU.add))
            own.done(nc.vector.tensor_scalar(rel[:, :], dst_f[:, :], dst_f[:, 0:1], None, ALU.subtract))
            own.mark(nc.vector.scalar_tensor_tensor(win[:, :], src_high[:, :], float(W), rel[:, :], ALU.mult, ALU.add))
            own.mark(nc.vector.tensor_reduce(small[0:G, 1:2], rel[:, :], AX.X, ALU.max))
            own.done(nc.vector.tensor_reduce(small[0:G, 2:3], rel[:, :], AX.X, ALU.min))
            own.done(nc.vector.tensor_scalar(small[0:G, 3:4], small[0:G, 1:2], float(W - 1), None, ALU.is_gt))
            nc.vector.scalar_tensor_tensor(small[0:G, 4:5], small[0:G, 2:3], 0.0, small[0:G, 3:4], ALU.is_lt, ALU.add).then_inc(edge_rows_ready, 1)
            dve.wait_ge(w_in, 16 * KC)
            dve.wait_ge(att_in, 32)
            for c in range(KC):
                for a in range(2):
                    own.done(nc.vector.tensor_tensor_reduce(out=junk_w[:, :], in0=Wraw[:, c, 0:D], in1=attb[:, a, :], scale=1.0, scalar=0.0,
                                                            op0=ALU.mult, op1=ALU.add, accum_out=Wraw[:, c, D + a:D + a + 1]))
            nc.vector.memset(small[:, 5:6], 0.0).then_inc(att_cols_ready, 1)
            dve.wait_ge(x_in, 64)
            for i in range(NT):
                for h in range(2):
                    last = nc.vector.bn_stats(bn[:, i, h, :], xall[:, i, h * HALF:(h + 1) * HALF])
            own.done(last)
            for i in range(NT):
                last = nc.vector.bn_aggr(mv[:, i, :], bn[:, i, :, :])
            own.done(last)
            own.mark(nc.vector.tensor_scalar(negmean[:, :], mv[:, :, 0], -1.0, None, ALU.mult))
            nc.vector.tensor_scalar(varep[:, :], mv[:, :, 1], LN_EPS, None, ALU.add).then_inc(stats_ready, 1)
            dve.wait_ge(consts_ready, 3)
            dve.wait_ge(countsT_zero, 1)
            dve.wait_ge(tables_ready, 1)
            dve.wait_ge(bases_in, 16)
            spread = dve.value_load(flag[0:1, 0:1], min_val=0, max_val=2 * G)
            with dve.If(spread == 0):
                def add_and_fill(i, b, fill=True):
                    q = i * PER_TILE + b
                    start = dve.value_load(bases[0:1, bass.ds(q, 1)], min_val=0, max_val=N - 1)
                    if fill:
                        onehots(q + LAG, (b + LAG) % RING)
                    dve.wait_ge(window_free, q + 2)
                    add_window(dve, q, b, start)

                for q in range(LAG):
                    onehots(q, q)
                with dve.Fori(0, NT - 1) as i:
                    for b in range(PER_TILE):
                        add_and_fill(i, b)
                for b in range(PER_TILE):
                    add_and_fill(NT - 1, b, fill=b + LAG < PER_TILE)
            with dve.Else():
                own_counts = Own(dve, dve_counts)
                dve.wait_ge(h_lo_ready, NT)
                own_counts.mark(nc.vector.tensor_scalar(tab_rel[:, :, :], tab_dst[:, :, :], float(W), None, ALU.add))
                with dve.Fori(0, WP) as w:
                    own_counts.wait()
                    kept = own_counts.enter(w, 6)
                    own_counts.done(nc.vector.tensor_scalar(tab_rel[:, :, :], tab_rel[:, :, :], float(-W), None, ALU.add))
                    own_counts.done(nc.vector.tensor_scalar(tab_ok[:, :, :], tab_rel[:, :, :], float(W - 1), None, ALU.is_le))
                    own_counts.done(nc.vector.scalar_tensor_tensor(tab_ok[:, :, :], tab_rel[:, :, :], 0.0, tab_ok[:, :, :], ALU.is_ge, ALU.mult))
                    own_counts.done(nc.vector.scalar_tensor_tensor(tab_to[:, :, :], tab_high[:, :, :], float(W), tab_rel[:, :, :], ALU.mult, ALU.add))
                    own_counts.done(nc.vector.scalar_tensor_tensor(tab_to[:, :, :], tab_to[:, :, :], 1.0, tab_ok[:, :, :], ALU.add, ALU.mult))
                    for c in range(2):
                        last = nc.vector.tensor_scalar(tab_win[:, :, :, c].rearrange("p g t -> p t g"), tab_to[:, :, :], -1.0, None, ALU.add)
                    own_counts.mark(last)
                    with dve.Fori(0, G // 2) as j:
                        own_counts.wait()
                        for b in range(2):
                            onehots(j * 2 + b, b)
                        for b in range(2):
                            q = w * G + j * 2 + b
                            dve.wait_ge(window_free, q + 2)
                            add_window(dve, q, b, w * W)
                    own_counts.leave(kept, WP)
            nc.vector.memset(small[:, 0:1], 0.0).then_inc(countsT_ready, 1)

            def attention_columns(n):
                c, a = n // 2, n % 2
                if n == 0:
                    dve.wait_ge(w2_in, 16 * KC)
                    dve.wait_ge(att2_in, 32)
                own.done(nc.vector.tensor_tensor_reduce(out=product[:, :], in0=Wraw2[:, c, 0:D], in1=attb2[:, a, :], scale=1.0, scalar=0.0,
                                                        op0=ALU.mult, op1=ALU.add, accum_out=Wraw2[:, c, D + a:D + a + 1]))

            for d in range(NT):
                dve.wait_ge(ct_conv, d + 1)
                nc.vector.tensor_tensor(ct_f[:, d % 2, d, :], ct_f[:, d % 2, d, :], ident[0:T, 0:T], ALU.add).then_inc(ct_diag, 1)
                attention_columns(d)
                if d >= 1:
                    put_counts(dve, d - 1)
            for n in range(NT, 2 * KC):
                attention_columns(n)
            nc.vector.memset(small[:, 6:7], 0.0).then_inc(att2_cols, 1)
            put_counts(dve, NT - 1)
            dve_attention(0, own)
            for s in range(0, NT, 2):
                dve.wait_ge(split_hi, s + 1)
                nc.vector.tensor_tensor(H[1][:, s, :], h_next[:, s, :], H[0][:, s, :].bitcast(F32), ALU.subtract).then_inc(split_dve, 1)
            dve_attention(1, own)
            dve_ffn(dve, own)

            def turned_low(i):
                dve.wait_ge(yt_hi, i + 1)
                dve.tensor_tensor(yT[1][:, i % 2, :, :], blocks(2 * (i % 2), KC)[:, :, 0:T], yT[0][:, i % 2, :, :].bitcast(F32), ALU.subtract).then_inc(yt_lo, 1)

            turned_low(0)
            for i in range(NT):
                if i + 1 < NT:
                    turned_low(i + 1)
                dve.wait_ge(proj_done, i + 1)
                dve.wait_ge(x2_plus, i + 1)
                if i >= 2:
                    dve.wait_ge(out_stored[i % 2], 32 * (i // 2))
                b = 4 + 2 * (i % 2)
                dve.tensor_tensor(out_sb[:, i % 2, :], PS[0:T, b:b + 2, :].rearrange("p b c -> p (b c)")[:, 0:D], x2_in[:, i % 2, :], ALU.add).then_inc(out_ready, 1)

        @block.tensor
        def _(pe):
            pe.wait_ge(consts_ready, 3)
            pe.wait_ge(edge_rows_ready, 1)
            for b, rows in enumerate((src_low, win, dst_f, src_high)):
                for t in range(ET):
                    nc.tensor.transpose(PS[0:T, b, t * G:(t + 1) * G], rows[:, t * T:(t + 1) * T], ident[0:G, 0:G])
            nc.tensor.matmul(bank(4, 1, 1), small[0:G, 4:5], ones[0:G, 0:1], start=True, stop=True).then_inc(edge_rows_turned, 1)

            def turn_rows(i):
                pe.wait_ge(xn_ready, i + 1)
                for k in range(KC):
                    last = nc.tensor.transpose(blocks(0, KC)[:, k, 0:T], xn[:, k * P:(k + 1) * P], ident[0:T, 0:T])
                last.then_inc(xn_turned, 1)

            def messages(i, part=0, parts=1):
                if part == 0:
                    pe.wait_ge(w_lo_ready, 1)
                    pe.wait_ge(xt_lo_ready, i + 1)
                    pe.wait_ge(h_free, i + 1)
                todo = [(h, n) for h in range(2) for n in range(3 * KC)]
                size = len(todo) // parts
                for h, n in todo[part * size:(part + 1) * size]:
                    lo, hi = ((0, HALF), (HALF, WX))[h]
                    (a, b), k = PARTS[n // KC], n % KC
                    last = nc.tensor.matmul(bank(5 + h, T, hi - lo), XT[a][:, k, :], Wg[b][:, k, lo:hi], start=(n == 0), stop=(n == 3 * KC - 1))
                if part == parts - 1:
                    last.then_inc(h_done, 1)

            def count(q, buf):
                pe.wait_ge(onehots_ready, q + 1)
                pe.wait_ge(window_free, q + 1)
                for t in range(ET):
                    last = nc.tensor.matmul(bank(3 + buf % 2, T, NT * W), oh_src[:, buf, t, 0:T], oh_win[:, buf, t, :], start=(t == 0), stop=(t == ET - 1))
                last.then_inc(group_counted, 1)

            pe.wait_ge(tables_ready, 1)
            spread = pe.value_load(flag[0:1, 0:1], min_val=0, max_val=2 * G)
            with pe.If(spread == 0):
                with pe.Fori(0, NT) as i:
                    for b in range(PER_TILE):
                        count(i * PER_TILE + b, b % RING)
                        if b == 0:
                            turn_rows(i)
                        if 3 <= b < 7:
                            messages(i, b - 3, 4)
            with pe.Else():
                with pe.Fori(0, NT) as i:
                    turn_rows(i)
                    messages(i)
                with pe.Fori(0, WP) as w:
                    with pe.Fori(0, G // 2) as j:
                        for b in range(2):
                            count(w * G + j * 2 + b, b)
            pe.wait_ge(h_free, NT + 1)
            for d in range(NT):
                pe.wait_ge(ct_diag, d + 1)
                if d >= 2:
                    pe.wait_ge(counts_ready, d - 1)
                for s in range(NT):
                    last = nc.tensor.transpose(blocks(3 * (d % 2), NT)[0:T, s, 0:T], ct_f[:, d % 2, s, :], ident[0:T, 0:T])
                last.then_inc(ct_turned, 1)
            pe.wait_ge(counts_ready, NT)
            pe_attention(0)
            pe_attention(1)
            pe_ffn(pe)

            def turn_last(i):
                pe.wait_ge(y_scaled, i + 1)
                if i == 0:
                    pe.wait_ge(group_free, len(USE))
                if i >= 2:
                    pe.wait_ge(yt_lo, i - 1)
                for k in range(KC):
                    last = pe.transpose(blocks(2 * (i % 2), KC)[:, k, 0:T], y_in[:, i % 2, k * P:(k + 1) * P], ident[0:T, 0:T])
                last.then_inc(y_turned, 1)

            def project(i):
                pe.wait_ge(yt_lo, i + 1)
                if i >= 2:
                    pe.wait_ge(out_ready, i - 1)
                b = 4 + 2 * (i % 2)
                to = PS[0:T, b:b + 2, :].rearrange("p b c -> p (b c)")
                for slot in range(3):
                    for m in range(3 * KC):
                        (x_, y_), k = PARTS[m // KC], m % KC
                        last = pe.matmul(to[:, slot * WB:(slot + 1) * WB], yT[x_][:, i % 2, k, :], Ws[y_][slot][:, k, 0:WB], start=(m == 0), stop=(m == 3 * KC - 1))
                last.then_inc(proj_done, 1)

            pe.wait_ge(ws_lo, BLOCKS + 3)
            turn_last(0)
            for i in range(NT):
                if i + 1 < NT:
                    turn_last(i + 1)
                project(i)


_INS = ("x", "src", "dst", "L0_gnn_W1", "L0_gnn_att_src1", "L0_gnn_att_dst1", "L0_gnn_b1", "L0_gnn_W2", "L0_gnn_att_src2",
        "L0_gnn_att_dst2", "L0_gnn_b2", "L0_ffn_Wqk", "L0_ffn_bqk", "L0_ffn_Wv", "L0_ffn_bv", "L0_ffn_conv_w", "L0_ffn_conv_b",
        "L0_ffn_glob", "L0_ffn_pos_bias", "L0_ffn_Wg1", "L0_ffn_bg1", "L0_ffn_Wg2", "L0_ffn_bg2", "L0_ffn_Wp", "L0_ffn_bp")


def kernel(**inputs):
    import numpy as _np
    import concourse.bacc as _bacc
    from concourse import mybir as _mybir
    from concourse.bass_utils import run_bass_kernel_spmd as _run

    nc = _bacc.Bacc("TRN2", target_bir_lowering=False, num_devices=1)
    arrays, a = {}, {}
    for name in _INS:
        v = _np.ascontiguousarray(inputs[name])
        arrays[f"in_{name}_dram"] = v
        a[name] = nc.dram_tensor(f"in_{name}_dram", v.shape, _mybir.dt.from_np(v.dtype), kind="ExternalInput").ap()
    out = nc.dram_tensor("out_dram", (N, D), F32, kind="ExternalOutput").ap()
    gnn = [{"W": a[f"L0_gnn_W{l}"], "as": a[f"L0_gnn_att_src{l}"], "ad": a[f"L0_gnn_att_dst{l}"], "b": a[f"L0_gnn_b{l}"]} for l in (1, 2)]
    ffn = {name[7:]: a[name] for name in _INS if name.startswith("L0_ffn_")}
    program(nc, a["x"], a["src"], a["dst"], gnn, ffn, out)
    return _run(nc, [arrays], core_ids=[0]).results[0]["out_dram"]
```

```python
import numpy as np
import concourse.bass as bass
from concourse import mybir
from contextlib import ExitStack

F32 = mybir.dt.float32
F32R = mybir.dt.float32r
BF16 = mybir.dt.bfloat16
FP16 = mybir.dt.float16
I32 = mybir.dt.int32
U16 = mybir.dt.uint16
BYTES = {F32: 4, F32R: 4, I32: 4, BF16: 2, FP16: 2, U16: 2}
ALU = mybir.AluOpType
ACT = mybir.ActivationFunctionType
AX = mybir.AxisListType

N = 1250
E = 40000
D = 768
HEADS = 3
HD = D // HEADS
GATE = 32
T = 125
NT = N // T
P = 128
KC = D // P
HALF = D // 2
HC = HD // P
G = 80
GE = E // G
ET = GE // T
W = 20
WP = (N + W - 1) // W
CTW = N + W
ACT_COLUMNS = 8
DVE_COLUMNS = 3
SHARES = 6
PER_TILE = G // NT
OHS = T + T % 2
RING = 4
WINDOW_BANKS = (2, 7)
EARLY = 7
LAG = RING - 1
WX = D + 2
LN_EPS = 1e-5
NEG_SLOPE = 0.2
FAR = -1e30
ROUND = 12582912.0
WB = HD
WG = WB + GATE
BLOCKS = 3 * HEADS
SPAN = ((0, 418), (418, 416), (834, 416))
BANK = 512
SCALE = HD ** -0.5
TURNED_PARTS = (slice(0, 4), slice(4, NT))
Y_LOADS = (range(0, 1), range(1, 3), range(3, 8), range(8, 9), range(9, 10))
PARTS = ((1, 0), (0, 1), (0, 0))
HIGH_FIRST = ((0, 0), (0, 1), (1, 0))


class Own:

    def __init__(self, eng, sem):
        self.eng, self.sem, self.base, self.n = eng, sem, 0, 0

    def mark(self, ins):
        ins.then_inc(self.sem, 1)
        self.n += 1

    def wait(self):
        self.eng.wait_ge(self.sem, self.base + self.n)

    def done(self, ins):
        self.mark(ins)
        self.wait()

    def enter(self, i, steps):
        kept = (self.base, self.n, steps)
        self.base, self.n = self.base + self.n + i * steps, 0
        return kept

    def leave(self, kept, times):
        base, n, steps = kept
        assert self.n == steps, (self.n, steps)
        self.base, self.n = base, n + times * steps


def program(nc, x, src, dst, gnn, ffn, out):
    ctx = ExitStack()
    with ctx:
        def sem(name):
            return ctx.enter_context(nc.semaphore(name))

        BASE, TOP = 16512, 229368
        tensors = {}

        def sb(name, shape, dt, offset):
            size = int(np.prod(shape[1:])) * BYTES[dt]
            assert offset % 4 == 0 and BASE + offset + size <= TOP, (name, offset, size)
            tensors[name] = (offset, size)
            return nc.alloc_sbuf_tensor_at(name, shape, dt, offset=BASE + offset)

        def after(name):
            o, s = tensors[name]
            return (o + s + 31) // 32 * 32

        ident = sb("ident", [P, P], F32, 0)
        ones = sb("ones", [P, P], F32, after("ident"))
        gate_scale = sb("gate_scale", [T, HEADS, NT], F32, after("ones"))
        asd = sb("asd", [T, NT, 2], F32, after("gate_scale"))
        ad_slope = sb("ad_slope", [T, NT], F32, after("asd"))
        rden = sb("rden", [T, NT], F32, after("ad_slope"))
        stat = sb("stat", [T, 8], F32, after("rden"))
        small = sb("small", [P, 8], F32, after("stat"))
        flag = sb("flag", [1, 1], I32, after("small"))
        H = [sb("H_hi", [T, NT, D], F32R, after("flag")), None]
        H[1] = sb("H_lo", [T, NT, D], F32R, after("H_hi"))
        counts = sb("counts", [T, NT, N], U16, after("H_lo"))
        Wg = [sb("W_hi", [P, KC, WX], F32R, after("counts")), None]
        Wg[1] = sb("W_lo", [P, KC, WX], F32R, after("W_hi"))
        XT = [sb("XT_hi", [P, KC, T], F32R, after("W_lo")), None]
        XT[1] = sb("XT_lo", [P, KC, T], F32R, after("XT_hi"))
        Wraw = sb("Wraw", [P, KC, WX], F32, tensors["counts"][0])

        xall = sb("xall", [T, NT, D], F32, after("XT_lo"))
        xn = sb("xn", [T, D], F32, after("xall"))
        xt_raw = sb("xt_raw", [P, KC, T], F32, after("xn"))
        h_raw = sb("h_raw", [T, WX], F32, after("xt_raw"))
        bn = sb("bn", [T, 2, 2, 6], F32, after("h_raw"))
        mv = sb("mv", [T, 2, 2], F32, after("bn"))
        rstd = sb("rstd", [T, NT], F32, after("mv"))
        negmean = sb("negmean", [T, NT], F32, after("rstd"))
        varep = sb("varep", [T, NT], F32, after("negmean"))
        shift = sb("shift", [T, NT], F32, after("varep"))
        minus_half = sb("minus_half", [T, NT], F32, after("shift"))
        oh_src = sb("oh_src", [T, RING, ET, OHS], BF16, after("minus_half"))
        oh_win = sb("oh_win", [T, RING, ET, NT * W], BF16, after("oh_src"))
        countsT = sb("countsT", [T, NT, CTW], U16, after("oh_win"))
        iota = sb("iota", [T, NT * W], FP16, after("countsT"))
        bases = sb("bases", [1, LAG + G], I32, after("iota"))
        junk_x = sb("junk_x", [P, D], BF16, after("bases"))
        sums = sb("sums", [T, NT], F32, after("junk_x"))
        mean_root = sb("mean_root", [T, NT], F32, after("sums"))
        eps = sb("eps", [T, 1], F32, after("mean_root"))
        place_i = sb("place_i", [G, 1], I32, after("eps"))
        place = sb("place", [G, 1], F32, after("place_i"))
        tab_low = sb("tab_low", [T, G, ET, 2], FP16, after("Wraw"))
        tab_win = sb("tab_win", [T, G, ET, 2], FP16, after("tab_low"))
        tab_dst = sb("tab_dst", [T, ET, G], F32, after("tab_win"))
        tab_high = sb("tab_high", [T, ET, G], F32, after("tab_dst"))
        e0 = tensors["H_hi"][0]
        dst_i = sb("dst_i", [G, GE], I32, e0)
        src_i = sb("src_i", [G, GE], I32, e0 + 4096)
        dst_f = sb("dst_f", [G, GE], F32, e0 + 2 * 4096)
        src_high = sb("src_high", [G, GE], F32, e0 + 3 * 4096)
        src_low = sb("src_low", [G, GE], F32, e0 + 4 * 4096)
        rel = sb("rel", [G, GE], F32, e0 + 5 * 4096)
        win = sb("win", [G, GE], F32, e0 + 6 * 4096)
        iota_i = sb("iota_i", [T, NT * W], I32, e0 + 7 * 4096)
        attb = sb("attb", [P, 2, D], F32, e0 + 8 * 4096)
        junk_w = sb("junk_w", [P, D], F32, e0 + 10 * 4096)
        tab_rel = sb("tab_rel", [T, ET, G], F32, tensors["h_raw"][0])
        tab_ok = sb("tab_ok", [T, ET, G], F32, after("tab_rel"))
        tab_to = sb("tab_to", [T, ET, G], F32, tensors["xt_raw"][0])
        ct_f = sb("ct_f", [T, 2, NT, T], F32, tensors["W_hi"][0])
        ct_early = sb("ct_early", [T, NT, T], F32, tensors["xall"][0])

        Wraw2 = sb("Wraw2", [P, KC, WX], F32, tensors["xall"][0])
        attb2 = sb("attb2", [P, 2, D], F32, after("Wraw2"))
        product = sb("product", [P, 2, D], F32, after("attb2"))
        h_next = sb("h_next", [T, NT, D], F32, tensors["xall"][0])
        asb = sb("asb", [T, NT, T], F32, max(after("xall"), after("product")))
        prob = sb("prob", [T, N], F32, after("asb"))
        far = sb("far", [T, N], BF16, after("prob"))
        junk = sb("junk", [T, N], BF16, after("far"))
        PT = [sb("PT_hi", [T, NT, T], F32R, after("junk")), None]
        PT[1] = sb("PT_lo", [T, NT, T], F32R, after("PT_hi"))
        rows = sb("rows", [T, D], F32, after("PT_lo"))
        bias_b = sb("bias_b", [T, D], F32, after("rows"))
        xnT = [sb("xnT_hi", [P, KC, N], F32R, tensors["W_hi"][0]), None]
        xnT[1] = sb("xnT_lo", [P, KC, N], F32R, after("xnT_hi"))
        x_plus = sb("x_plus", [T, D], F32, after("xnT_lo"))
        xn2 = sb("xn2", [T, D], F32, after("x_plus"))
        bn2 = sb("bn2", [T, 2, 6], F32, after("xn2"))
        mv2 = sb("mv2", [T, 2], F32, after("bn2"))
        ln2 = sb("ln2", [T, 4], F32, after("mv2"))
        half2 = sb("half2", [T, 1], F32, after("ln2"))
        assert after("half2") <= tensors["asb"][0]

        qT = [sb("qT_hi", [P, HC, N], F32R, tensors["H_hi"][0]), None]
        qT[1] = sb("qT_lo", [P, HC, N], F32R, after("qT_hi"))
        kT = [sb("kT_hi", [P, HC, N], F32R, after("qT_lo")), None]
        kT[1] = sb("kT_lo", [P, HC, N], F32R, after("kT_hi"))
        vs = [sb("v_hi", [T, NT, HD], F32R, after("kT_lo")), None]
        vs[1] = sb("v_lo", [T, NT, HD], F32R, after("v_hi"))
        q_raw = sb("q_raw", [P, HC, N + 2], F32, after("v_lo"))
        tri = sb("tri", [T, T], F32, after("q_raw"))
        bqk_c = sb("bqk_c", [P, 2 * KC], F32, after("tri"))
        conv_wc = sb("conv_wc", [P, HC, 3], F32, after("bqk_c"))
        conv_bc = sb("conv_bc", [P, HC], F32, after("conv_wc"))
        bg1_b = sb("bg1_b", [T, GATE], F32, after("conv_bc"))
        bg2_b = sb("bg2_b", [T, HEADS], F32, after("bg1_b"))
        wg2_b = sb("wg2_b", [T, GATE, HEADS], F32, after("bg2_b"))
        bv_b = sb("bv_b", [T, D], F32, after("wg2_b"))
        gate_h = sb("gate_h", [T, NT, GATE], F32, after("bv_b"))
        gate_t = sb("gate_t", [T, NT, GATE], F32, after("gate_h"))
        gate_e = sb("gate_e", [T, HEADS, NT], F32, after("gate_t"))
        gate_c = sb("gate_c", [T, 4, NT], F32, after("gate_e"))
        att_max = sb("att_max", [T, 4], F32, after("gate_c"))
        att_den = sb("att_den", [T, 4], F32, after("att_max"))
        ys_out = sb("ys_out", [T, 2, HD], F32, after("att_den"))
        assert after("ys_out") <= tensors["xnT_hi"][0]
        pexp = sb("pexp", [P, N], F32, after("xnT_lo"))
        w_raw = sb("w_raw", [P, KC, WG], F32, after("half2"))
        Ws = [[None] * 3, [None] * 3]
        Ws[0][1] = sb("Ws_k_hi", [P, KC, WB], F32R, after("w_raw"))
        Ws[1][1] = sb("Ws_k_lo", [P, KC, WB], F32R, after("Ws_k_hi"))
        Ws[0][2] = sb("Ws_v_hi", [P, KC, WG], F32R, after("Ws_k_lo"))
        Ws[1][2] = sb("Ws_v_lo", [P, KC, WG], F32R, after("Ws_v_hi"))
        pT = [sb("pT_hi", [T, NT, T], F32R, after("Ws_v_lo")), None]
        pT[1] = sb("pT_lo", [T, NT, T], F32R, after("pT_hi"))
        Ws[0][0] = sb("Ws_q_hi", [P, KC, WB], F32R, max(after("pT_lo"), after("bias_b")))
        Ws[1][0] = sb("Ws_q_lo", [P, KC, WB], F32R, after("Ws_q_hi"))
        assert after("pexp") <= tensors["w_raw"][0] and after("w_raw") <= tensors["asb"][0]
        y_in = sb("y_in", [T, NT, D], F32, tensors["xnT_hi"][0])
        x2_in = sb("x2_in", [T, NT - 1, D], F32, after("y_in"))
        assert after("x2_in") <= tensors["pexp"][0]
        yT = [sb("yT_hi", [P, 2, KC, T], F32R, tensors["qT_hi"][0]), None]
        yT[1] = sb("yT_lo", [P, 2, KC, T], F32R, after("yT_hi"))
        out_sb = sb("out_sb", [T, 2, D], F32, after("yT_lo"))
        x2_last = sb("x2_last", [T, D], F32, after("out_sb"))
        assert after("x2_last") <= tensors["v_hi"][0]
        bp_b = sb("bp_b", [T, D], F32, tensors["q_raw"][0])

        PS = ctx.enter_context(nc.psum_tensor("PS", [P, 8, 512], F32))

        def blocks(bank, n):
            return PS[:, bank:bank + (n + 3) // 4, :].rearrange("p b (q c) -> p (b q) c", c=P)[:, 0:n, :]

        def bank(b, rows, cols):
            return PS[0:rows, b, 0:cols]

        edges_in, bases_in, x_in, w_in, att_in = (sem(s) for s in
            ("edges_in", "bases_in", "x_in", "w_in", "att_in"))
        dve_counts = sem("dve_counts")
        pool_own, dve_own = sem("pool_own"), sem("dve_own")
        consts_ready = sem("consts_ready")
        edge_rows_ready, edge_rows_turned, tables_ready = sem("edge_rows_ready"), sem("edge_rows_turned"), sem("tables_ready")
        x_head_in, stats_ready, sums_ready, means_ready, squares_ready, rstd_ready = (sem(s) for s in
            ("x_head_in", "stats_ready", "sums_ready", "means_ready", "squares_ready", "rstd_ready"))
        att_cols_ready = sem("att_cols_ready")
        w_hi_ready, w_lo_ready, att_hi_ready = sem("w_hi_ready"), sem("w_lo_ready"), sem("att_hi_ready")
        xn_ready, xn_turned, xt_raw_ready, xt_hi_ready, xt_lo_ready = (sem(s) for s in
            ("xn_ready", "xn_turned", "xt_raw_ready", "xt_hi_ready", "xt_lo_ready"))
        h_free = sem("h_free")
        h_done, h_hi_ready, h_lo_ready = (sem(s) for s in
            ("h_done", "h_hi_ready", "h_lo_ready"))
        onehots_ready, group_counted, window_free = (sem(s) for s in
            ("onehots_ready", "group_counted", "window_free"))
        countsT_filled, countsT_ready = sem("countsT_filled"), sem("countsT_ready")
        ct_conv, ct_turned, counts_ready = (sem(s) for s in
            ("ct_conv", "ct_turned", "counts_ready"))
        early_conv, early_turned, early_put = (sem(s) for s in ("early_conv", "early_turned", "early_put"))
        terms_in = sem("terms_in")
        w2_in, att2_in, product_ready, att2_act, att2_dve, w2_hi, w2_lo = (sem(s) for s in
            ("w2_in", "att2_in", "product_ready", "att2_act", "att2_dve", "w2_hi", "w2_lo"))
        split_hi, split_dve, split_pool = (sem(s) for s in ("split_hi", "split_dve", "split_pool"))
        half_ready, x_again, x_plus_ready, x2_stored, var_ready, ln_ready, xn2_ready = (sem(s) for s in
            ("half_ready", "x_again", "x_plus_ready", "x2_stored", "var_ready", "ln_ready", "xn2_ready"))
        LAYER = [{name: sem(f"{name}_{l}") for name in (
            "bias_in", "slope_ready", "asb_turned", "asb_ready", "line_ready", "arg_ready", "exp_ready",
            "probs_ready", "probs_turned", "pt_hi", "pt_lo", "rows_done", "rows_out", "rows_turned",
            "xt_hi", "xt_lo", "msgs_done", "msgs_out")} for l in range(2)]
        ws_in, ws_hi, ws_lo, tabs_in, tri_ready = (sem(s) for s in ("ws_in", "ws_hi", "ws_lo", "tabs_in", "tri_ready"))
        group_done, group_hi, group_free, conv_ready, conv_hi = (sem(s) for s in
            ("group_done", "group_hi", "group_free", "conv_ready", "conv_hi"))
        scores_done, max_ready, pexp_ready, pexp_turned, pexp_hi, pexp_lo = (sem(s) for s in
            ("scores_done", "max_ready", "pexp_ready", "pexp_turned", "pexp_hi", "pexp_lo"))
        gate_arg, gate_exp, gate_ready = (sem(s) for s in ("gate_arg", "gate_exp", "gate_ready"))
        ys_stored = [sem("ys_stored_even"), sem("ys_stored_odd")]
        y_loaded = [sem(f"y_loaded_{n}") for n in range(len(Y_LOADS))]
        x2_loaded = [sem("x2_loaded"), sem("x2_last_loaded")]
        out_stored = [sem("out_stored_even"), sem("out_stored_odd")]
        bp_in, y_scaled, y_turned, yt_hi, yt_lo, x2_plus, proj_done, out_ready = (sem(s) for s in
            ("bp_in", "y_scaled", "y_turned", "yt_hi", "yt_lo", "x2_plus", "proj_done", "out_ready"))
        y_dram = nc.dram_tensor("y_scratch", [N, D], F32).ap()
        x2_dram = nc.dram_tensor("x2_scratch", [N, D], F32).ap()

        block = ctx.enter_context(nc.Block())

        def rows_in(eng, to, frm, s):
            eng.dma_start(to[0:120], frm[0:120]).then_inc(s, 16)
            eng.dma_start(to[120:T], frm[120:T]).then_inc(s, 16)

        def rows_out_to(eng, to, frm, s):
            eng.dma_start(to[0:120], frm[0:120, :]).then_inc(s, 16)
            eng.dma_start(to[120:T], frm[120:T, :]).then_inc(s, 16)

        def act_terms(l):
            L = LAYER[l]
            if l == 0:
                nc.scalar.wait_ge(h_lo_ready, NT)
            nc.scalar.wait_ge(L["asb_turned"], 1)
            nc.scalar.activation(asb[:, :, :], blocks(0, NT)[0:T, :, 0:T], ACT.Copy).then_inc(L["asb_ready"], 1)

        def act_first_line(l):
            nc.scalar.wait_ge(LAYER[l]["asb_ready"], 1)
            nc.scalar.wait_ge(LAYER[l]["slope_ready"], 1)
            act_slope_line(l, 0)

        def act_slope_line(l, d):
            L = LAYER[l]
            nc.scalar.activation(prob[:, :], asb[:, :, :].rearrange("p a b -> p (a b)"), ACT.Identity,
                                 bias=ad_slope[:, bass.ds(d, 1)], scale=NEG_SLOPE).then_inc(L["line_ready"], 1)

        def act_exp_edges(l, d):
            L = LAYER[l]
            nc.scalar.wait_ge(L["arg_ready"], d + 1)
            nc.scalar.activation(prob[:, :], prob[:, :], ACT.Exp).then_inc(L["exp_ready"], 1)

        def act_line(l, d):
            nc.scalar.wait_ge(LAYER[l]["probs_turned"], 2 * d)
            act_slope_line(l, d)
            act_exp_edges(l, d)

        def act_probs_high(l, d):
            L = LAYER[l]
            for h, part in enumerate(TURNED_PARTS):
                nc.scalar.wait_ge(L["probs_turned"], 2 * d + 1 + h)
                nc.scalar.activation(PT[0][:, part, :], blocks(0, NT)[0:T, part, 0:T], ACT.Copy).then_inc(L["pt_hi"], 1)

        def act_rows_high(l, d):
            L = LAYER[l]
            if l == 0:
                nc.scalar.wait_ge(L["rows_turned"], d + 1)
                nc.scalar.activation(XT[0][:, :, :], blocks(0, KC)[:, :, 0:T], ACT.Relu).then_inc(L["xt_hi"], 1)
            else:
                nc.scalar.wait_ge(L["rows_turned"], d + 1)
                nc.scalar.activation(xnT[0][:, :, bass.ds(d * T, T)], blocks(row_bank(l, d), KC)[:, :, 0:T], ACT.Copy).then_inc(L["xt_hi"], 1)

        def act_normalise(d):
            nc.scalar.wait_ge(ln_ready, d + 1)
            nc.scalar.activation(xn2[:, :], rows[:, :], ACT.Identity, bias=ln2[:, 3:4], scale=ln2[:, 2:3]).then_inc(xn2_ready, 1)

        def act_next_second_half(d):
            nc.scalar.wait_ge(LAYER[0]["msgs_done"], 2 * d + 1)
            nc.scalar.activation(asd[:, bass.ds(d, 1), :].rearrange("p a b -> p (a b)"), PS[0:T, 6, HALF:HALF + 2], ACT.Copy).then_inc(terms_in, 1)
            nc.scalar.activation(h_next[:, bass.ds(d, 1), HALF:D].rearrange("p a d -> p (a d)"), bank(6, T, HALF), ACT.Copy)

        def act_next_first_half(d):
            nc.scalar.wait_ge(LAYER[0]["msgs_done"], 2 * d + 2)
            nc.scalar.activation(h_next[:, bass.ds(d, 1), 0:HALF].rearrange("p a d -> p (a d)"), bank(5, T, HALF), ACT.Copy).then_inc(LAYER[0]["msgs_out"], 1)

        def act_messages_next(d):
            act_next_second_half(d)
            act_next_first_half(d)

        def act_split(s):
            nc.scalar.wait_ge(LAYER[0]["msgs_out"], s + 2)
            nc.scalar.activation(H[0][:, s, :], h_next[:, s, :], ACT.Copy).then_inc(split_hi, 1)

        def act_second_weight(h):
            half = slice(h * KC // 2, (h + 1) * KC // 2)
            nc.scalar.activation(Wg[0][:, half, :], Wraw2[:, half, :], ACT.Copy).then_inc(w2_hi, 1)

        def act_column(n):
            c, a = n // 2, n % 2
            nc.scalar.wait_ge(product_ready, n + 1)
            nc.scalar.activation(product[:, a, :], product[:, a, :], ACT.Copy, accum_out=Wraw2[:, c, D + a:D + a + 1]).then_inc(att2_act, 1)

        def act_attention(l):
            L = LAYER[l]
            act = nc.scalar
            if l == 1:
                act_split(NT - 1)
                act_exp_edges(l, 0)
            act_probs_high(l, 0)
            act.wait_ge(L["probs_turned"], 2)
            act_slope_line(l, 1)
            if l == 0:
                for n in range(2, ACT_COLUMNS - 2):
                    act_column(n)
            act_exp_edges(l, 1)
            if l == 0:
                act_column(ACT_COLUMNS - 2)
                act_column(ACT_COLUMNS - 1)
            act_probs_high(l, 1)
            act.wait_ge(L["probs_turned"], 4)
            act_slope_line(l, 2)
            if l == 0:
                act.wait_ge(att2_act, ACT_COLUMNS)
                act.wait_ge(att2_dve, 1)
                act_second_weight(0)
                act_second_weight(1)
            act_exp_edges(l, 2)
            if l == 0:
                act_rows_high(l, 0)
                with act.Fori(1, NT - 2) as d:
                    act_probs_high(l, d + 1)
                    act_line(l, d + 2)
                    act_messages_next(d - 1)
                    act_rows_high(l, d)
                act_probs_high(l, NT - 1)
                act_messages_next(NT - 3)
                act_rows_high(l, NT - 2)
                act.wait_ge(L["rows_done"], 2 * NT)
                for s in range(NT - 4):
                    act_split(s)
                act_messages_next(NT - 2)
                act_rows_high(l, NT - 1)
                for s in range(NT - 4, NT - 1):
                    act_split(s)
                act_next_second_half(NT - 1)
                act_terms(1)
                act_first_line(1)
                act_next_first_half(NT - 1)
            else:
                act_normalise(0)
                act_weight(0)
                with act.Fori(1, NT - 2) as d:
                    act_probs_high(l, d + 1)
                    act_line(l, d + 2)
                    act_rows_high(l, d - 1)
                    act_normalise(d)
                act_probs_high(l, NT - 1)
                for d in (NT - 2, NT - 1):
                    act_rows_high(l, d - 1)
                    act_normalise(d)

        def counts_of(d):
            return counts[:, bass.ds(d, 1), :].rearrange("p a b -> p (a b)")

        def dve_args(l, d, own):
            L, dve, cnt = LAYER[l], nc.vector, counts_of(d)
            ad = asd[:, bass.ds(d, 1), 1:2].rearrange("p a b -> p (a b)")
            src = asb[:, :, :].rearrange("p a b -> p (a b)")
            own.done(dve.tensor_scalar(far[:, :], cnt, 0.0, FAR, ALU.is_equal, ALU.mult))
            if isinstance(d, int) and d == 0:
                dve.wait_ge(L["asb_ready"], 1)
            own.mark(dve.memset(stat[:, 5:6], 0.0))
            own.done(dve.tensor_tensor_reduce(out=junk[:, :], in0=src, in1=far[:, :], scale=1.0, scalar=-3e38, op0=ALU.add, op1=ALU.max, accum_out=stat[:, 0:1]))
            own.done(dve.tensor_scalar(stat[:, 1:2], stat[:, 0:1], ad, None, ALU.add))
            own.mark(dve.scalar_tensor_tensor(stat[:, 2:3], stat[:, 1:2], NEG_SLOPE, stat[:, 1:2], ALU.mult, ALU.max))
            dve.wait_ge(L["line_ready"], d + 1)
            own.done(dve.scalar_tensor_tensor(prob[:, :], src, ad, prob[:, :], ALU.add, ALU.max))
            dve.tensor_scalar(prob[:, :], prob[:, :], stat[:, 2:3], 0.0, ALU.subtract, ALU.min).then_inc(L["arg_ready"], 1)

        def dve_numerators(l, d, own):
            L, dve = LAYER[l], nc.vector
            dve.wait_ge(L["exp_ready"], d + 1)
            dve.scalar_tensor_tensor(prob[:, :], prob[:, :], 1.0, counts_of(d), ALU.mult, ALU.mult, accum_out=stat[:, 3:4]).then_inc(L["probs_ready"], 1)
            dve.wait_ge(L["probs_ready"], d + 1)
            own.done(dve.reciprocal(rden[:, bass.ds(d, 1)], stat[:, 3:4]))

        def dve_probs(l, d, own, stats_of=None):
            dve_args(l, d, own)
            if stats_of is not None:
                dve_row_stats(stats_of, own)
            dve_numerators(l, d, own)

        PROB_STEPS = 7

        def dve_probs_low(l, d):
            L, dve = LAYER[l], nc.vector
            dve.wait_ge(L["pt_hi"], 2 * d + 2)
            dve.tensor_tensor(PT[1][:, :, :], blocks(0, NT)[0:T, :, 0:T], PT[0][:, :, :].bitcast(F32), ALU.subtract).then_inc(L["pt_lo"], 1)

        def dve_rows_out(l, d):
            L, dve = LAYER[l], nc.vector
            if l == 1:
                dve.wait_ge(x_plus_ready, d + 1)
                if not isinstance(d, int) or d >= 1:
                    dve.wait_ge(x2_stored, d * 32)
                    dve.wait_ge(xn2_ready, d)
            other = bias_b if l == 0 else x_plus
            for h in range(2):
                part = slice(h * HALF, (h + 1) * HALF)
                dve.wait_ge(L["rows_done"], 2 * d + 1 + h)
                dve.scalar_tensor_tensor(rows[:, part], bank(3 + h, T, HALF), rden[:, bass.ds(d, 1)], other[:, part], ALU.mult, ALU.add).then_inc(L["rows_out"], 1)

        def dve_row_stats(d, own):
            dve = nc.vector
            dve.wait_ge(LAYER[1]["rows_out"], 2 * d + 2)
            for h in range(2):
                last = dve.bn_stats(bn2[:, h, :], rows[:, h * HALF:(h + 1) * HALF])
            own.done(last)
            own.mark(dve.memset(stat[:, 6:7], 0.0))
            own.done(dve.bn_aggr(mv2[:, :], bn2[:, :, :]))
            dve.tensor_scalar(ln2[:, 0:1], mv2[:, 0:1], -1.0, None, ALU.mult)
            dve.tensor_scalar(ln2[:, 1:2], mv2[:, 1:2], LN_EPS, None, ALU.add).then_inc(var_ready, 1)
        STAT_STEPS = 3

        def dve_rows_low(l, d):
            L, dve = LAYER[l], nc.vector
            dve.wait_ge(L["xt_hi"], d + 1)
            src = blocks(row_bank(l, d), KC)[:, :, 0:T]
            if l == 0:
                dve.scalar_tensor_tensor(XT[1][:, :, :], src, 0.0, XT[0][:, :, :].bitcast(F32), ALU.max, ALU.subtract).then_inc(L["xt_lo"], 1)
            else:
                at = bass.ds(d * T, T)
                dve.tensor_tensor(xnT[1][:, :, at], src, xnT[0][:, :, at].bitcast(F32), ALU.subtract).then_inc(L["xt_lo"], 1)

        def attention_column(n, own):
            c, a = n // 2, n % 2
            own.done(nc.vector.tensor_tensor_reduce(out=junk_x[:, :], in0=Wraw2[:, c, 0:D], in1=attb2[:, a, :], scale=1.0, scalar=0.0,
                                                    op0=ALU.mult, op1=ALU.add, accum_out=Wraw2[:, c, D + a:D + a + 1]))

        def dve_slope(l):
            nc.vector.tensor_scalar(ad_slope[:, :], asd[:, :, 1], NEG_SLOPE, None, ALU.mult).then_inc(LAYER[l]["slope_ready"], 1)

        def dve_attention(l, own):
            L, dve = LAYER[l], nc.vector
            if l == 1:
                dve.wait_ge(terms_in, NT)
                dve_slope(l)
                dve_probs(l, 0, own)
            dve_probs_low(l, 0)
            dve_args(l, 1, own)
            if l == 0:
                attention_column(2 * KC - 1, own)
                dve.memset(stat[:, 6:7], 0.0).then_inc(att2_dve, 1)
            dve_numerators(l, 1, own)
            dve.wait_ge(L["bias_in"], 16)
            if l == 0:
                dve_rows_out(l, 0)
                dve_probs_low(l, 1)
                dve_probs(l, 2, own)
                dve_rows_low(l, 0)
                with dve.Fori(1, NT - 2) as d:
                    kept = own.enter(d - 1, PROB_STEPS)
                    dve_rows_out(l, d)
                    dve_probs_low(l, d + 1)
                    dve_probs(l, d + 2, own)
                    dve_rows_low(l, d)
                    own.leave(kept, NT - 3)
                dve_rows_out(l, NT - 2)
                dve_probs_low(l, NT - 1)
                dve_rows_low(l, NT - 2)
                dve_rows_out(l, NT - 1)
                dve_rows_low(l, NT - 1)
            else:
                dve_rows_out(l, 0)
                dve_probs_low(l, 1)
                dve_probs(l, 2, own, stats_of=0)
                with dve.Fori(1, NT - 2) as d:
                    kept = own.enter(d - 1, PROB_STEPS + STAT_STEPS)
                    dve_rows_out(l, d)
                    dve_probs_low(l, d + 1)
                    dve_probs(l, d + 2, own, stats_of=d)
                    dve_rows_low(l, d - 1)
                    own.leave(kept, NT - 3)
                dve_rows_out(l, NT - 2)
                dve_probs_low(l, NT - 1)
                dve_row_stats(NT - 2, own)
                dve_rows_low(l, NT - 3)
                dve_rows_out(l, NT - 1)
                dve_row_stats(NT - 1, own)
                dve_rows_low(l, NT - 2)

        def row_bank(l, d):
            return 5 if l == 1 and not (isinstance(d, int) and d >= NT - 2) else 0

        def pe_terms(l):
            for s in range(NT):
                last = nc.tensor.transpose(blocks(0, NT)[0:T, s, 0:T], asd[:, s, 0:1].to_broadcast([T, T]), ident[0:T, 0:T])
            last.then_inc(LAYER[l]["asb_turned"], 1)

        def pe_attention(l):
            L, pe = LAYER[l], nc.tensor

            def turn_probs(d):
                pe.wait_ge(L["probs_ready"], d + 1)
                if isinstance(d, int) and d == 0:
                    pe.wait_ge(L["asb_ready"], 1)
                if l == 0 and (not isinstance(d, int) or d >= 2):
                    pe.wait_ge(L["xt_lo"], d - 1)
                for s in range(NT):
                    last = pe.transpose(blocks(0, NT)[0:T, s, 0:T], prob[:, s * T:(s + 1) * T], ident[0:T, 0:T])
                    if s + 1 in (TURNED_PARTS[0].stop, NT):
                        last.then_inc(L["probs_turned"], 1)

            def mix(d):
                pe.wait_ge(L["pt_hi"], 2 * d + 1)
                for h in range(2):
                    if not isinstance(d, int) or d >= 1:
                        pe.wait_ge(L["rows_out"], 2 * d - 1 + h)
                    for n in range(3 * NT):
                        if h == 0 and n == TURNED_PARTS[1].start:
                            pe.wait_ge(L["pt_hi"], 2 * d + 2)
                        if h == 0 and n == 2 * NT:
                            pe.wait_ge(L["pt_lo"], d + 1)
                        (a, b), s = HIGH_FIRST[n // NT], n % NT
                        last = pe.matmul(bank(3 + h, T, HALF), PT[a][:, s, :], H[b][:, s, h * HALF:(h + 1) * HALF], start=(n == 0), stop=(n == 3 * NT - 1))
                    last.then_inc(L["rows_done"], 1)

            def turn_out(d, n):
                src = rows if l == 0 else xn2
                if l == 0:
                    pe.wait_ge(L["rows_out"], 2 * d + 2)
                    pe.wait_ge(L["pt_lo"], n)
                else:
                    pe.wait_ge(xn2_ready, d + 1)
                    if not isinstance(d, int) or d >= 1:
                        pe.wait_ge(L["xt_lo"], d)
                for k in range(KC):
                    last = pe.transpose(blocks(row_bank(l, d), KC)[:, k, 0:T], src[:, k * P:(k + 1) * P], ident[0:T, 0:T])
                last.then_inc(L["rows_turned"], 1)

            def next_messages(d):
                if l == 1:
                    return
                pe.wait_ge(w2_lo, 2)
                pe.wait_ge(L["xt_hi"], d + 1)
                pe.wait_ge(L["msgs_out"], d + 1)
                for h, (lo, hi) in ((1, (HALF, WX)), (0, (0, HALF))):
                    for n in range(3 * KC):
                        if (h, n) == (1, 2 * KC):
                            pe.wait_ge(L["xt_lo"], d + 1)
                        if (h, n) == (0, KC) and isinstance(d, int) and d == NT - 1:
                            pe.wait_ge(terms_in, NT)
                            pe_terms(1)
                        (a, b), k = HIGH_FIRST[n // KC], n % KC
                        last = pe.matmul(bank(5 + h, T, hi - lo), XT[a][:, k, :], Wg[b][:, k, lo:hi], start=(n == 0), stop=(n == 3 * KC - 1))
                    last.then_inc(L["msgs_done"], 1)

            turn_probs(0)
            if l == 0:
                pe.wait_ge(counts_ready, NT - EARLY)
            else:
                pe.wait_ge(split_dve, NT // 2)
                pe.wait_ge(split_pool, NT // 2)
            mix(0)
            turn_probs(1)
            if l == 0:
                turn_out(0, 2)
                with pe.Fori(1, NT - 1) as d:
                    mix(d)
                    turn_probs(d + 1)
                    next_messages(d - 1)
                    turn_out(d, d + 2)
                mix(NT - 1)
                next_messages(NT - 2)
                turn_out(NT - 1, NT)
                next_messages(NT - 1)
            else:
                mix(1)
                turn_probs(2)
                turn_out(0, 0)
                with pe.Fori(2, NT - 1) as d:
                    mix(d)
                    turn_probs(d + 1)
                    turn_out(d - 1, 0)
                mix(NT - 1)
                turn_out(NT - 2, 0)
                pe_columns("q", 0, range(0, HC))
                turn_out(NT - 1, 0)

        order = []
        for e in range(HEADS):
            if e == 0:
                order += [("q", e, n) for n in range(HC * 3)]
            order += [("k", e, n) for n in range(HC * 3)] + [("v", e, 0)]
            for i in range(NT):
                if i + 1 < NT:
                    order.append(("v", e, i + 1))
                elif e + 1 < HEADS:
                    order += [("q", e + 1, n) for n in range(HC * 3)]
                order.append(("y", e, i))
        USE = {key: n for n, key in enumerate(order)}
        HIGH = {key: n for n, key in enumerate(k for k in order if k[0] != "y" and k[:2] != ("q", 0))}

        def column_group(n):
            c, (start, size) = n % HC, SPAN[n // HC]
            return c, start, size

        def bias_col(kind, e, c):
            col = (KC if kind == "k" else 0) + e * HC + c
            return bqk_c[:, col:col + 1]

        def seen(i):
            return (i + 1) * T

        def pe_group(key):
            u = USE[key]
            if u >= 2:
                nc.tensor.wait_ge(group_free, u - 1)
            return 6 + u % 2

        def pe_columns(kind, e, groups=range(HC * 3)):
            slot = "qk".index(kind)
            nc.tensor.wait_ge(ws_lo, 3 * e + slot + 1)
            for n in groups:
                b = pe_group((kind, e, n))
                c, start, size = column_group(n)
                for m in range(3 * KC):
                    (x_, y_), k = PARTS[m // KC], m % KC
                    last = nc.tensor.matmul(bank(b, P, size), Ws[x_][slot][:, k, c * P:(c + 1) * P], xnT[y_][:, k, start:start + size],
                                            start=(m == 0), stop=(m == 3 * KC - 1))
                last.then_inc(group_done, 1)

        def pe_values(e, i):
            width = WG if e == 0 else HD
            nc.tensor.wait_ge(ws_lo, 3 * e + 3)
            b = pe_group(("v", e, i))
            for m in range(3 * KC):
                (x_, y_), k = PARTS[m // KC], m % KC
                last = nc.tensor.matmul(bank(b, T, width), xnT[x_][:, k, i * T:(i + 1) * T], Ws[y_][2][:, k, 0:width], start=(m == 0), stop=(m == 3 * KC - 1))
            last.then_inc(group_done, 1)

        def pe_scores(e, i):
            if i == 0:
                nc.tensor.wait_ge(group_free, USE["k", e, HC * 3 - 1] + 1)
            if e or i:
                nc.tensor.wait_ge(pexp_ready, e * NT + i)
            width = seen(i) + seen(i) % 2
            for j in range(0, width, BANK):
                size = min(BANK, width - j)
                for m in range(3 * HC):
                    (x_, y_), c = PARTS[m // HC], m % HC
                    last = nc.tensor.matmul(bank(j // BANK, T, size), qT[x_][:, c, i * T:(i + 1) * T], kT[y_][:, c, j:j + size], start=(m == 0), stop=(m == 3 * HC - 1))
            last.then_inc(scores_done, 1)

        def pe_turn(e, i):
            t = e * NT + i
            nc.tensor.wait_ge(pexp_ready, t + 1)
            if t:
                nc.tensor.wait_ge(pexp_lo, t)
            for s in range(i + 1):
                last = nc.tensor.transpose(blocks(3, NT)[0:T, s, 0:T], pexp[0:T, s * T:(s + 1) * T], ident[0:T, 0:T])
            last.then_inc(pexp_turned, 1)

        def pe_weighted(e, i):
            b = pe_group(("y", e, i))
            nc.tensor.wait_ge(pexp_lo, e * NT + i + 1)
            nc.tensor.wait_ge(group_free, USE["v", e, i] + 1)
            for m in range(3 * (i + 1)):
                (x_, y_), s = PARTS[m // (i + 1)], m % (i + 1)
                last = nc.tensor.matmul(bank(b, T, HD), pT[x_][:, s, :], vs[y_][:, s, :], start=(m == 0), stop=(m == 3 * (i + 1) - 1))
            last.then_inc(group_done, 1)

        def turn_last(i):
            nc.tensor.wait_ge(y_scaled, i + 1)
            if i >= 2:
                nc.tensor.wait_ge(yt_lo, i - 1)
            for k in range(KC):
                last = nc.tensor.transpose(blocks(2 * (i % 2), KC)[:, k, 0:T], y_in[:, i, k * P:(k + 1) * P], ident[0:T, 0:T])
            last.then_inc(y_turned, 1)

        def pe_ffn(pe):
            pe_columns("q", 0, range(HC, 2 * HC))
            pe.wait_ge(LAYER[1]["xt_lo"], NT)
            pe_columns("q", 0, range(2 * HC, 3 * HC))
            for e in range(HEADS):
                pe_columns("k", e)
                pe_values(e, 0)
                pe_scores(e, 0)
                for i in range(NT):
                    pe_turn(e, i)
                    if i + 1 < NT:
                        pe_scores(e, i + 1)
                        pe_values(e, i + 1)
                    elif e + 1 < HEADS:
                        pe_columns("q", e + 1)
                    else:
                        turn_last(0)
                    pe_weighted(e, i)

        def act_weight(b):
            width = WG if b == 2 else WB
            nc.scalar.wait_ge(ws_in, 16 * (b + 1 + (b >= 2)))
            if b >= 3:
                e, kind = (b - 3) // 3, "qkv"[b % 3]
                nc.scalar.wait_ge(group_done, USE[kind, e, (NT if kind == "v" else HC * 3) - 1] + 1)
            nc.scalar.activation(Ws[0][b % 3][:, :, 0:width], w_raw[:, :, 0:width], ACT.Copy).then_inc(ws_hi, 1)

        def act_column_group(kind, e, n):
            to = (qT if kind == "q" else kT)[0]
            c, start, size = column_group(n)
            u = USE[kind, e, n]
            nc.scalar.wait_ge(group_done, u + 1)
            nc.scalar.activation(to[:, c, start:start + size], bank(6 + u % 2, P, size), ACT.Identity, bias=bias_col(kind, e, c)).then_inc(group_hi, 1)

        def act_columns(kind, e):
            for n in range(HC * 3):
                act_column_group(kind, e, n)

        def act_conv_high(c):
            nc.scalar.wait_ge(conv_ready, c + 1)
            nc.scalar.activation(qT[0][:, c, :], pexp[:, :], ACT.Copy).then_inc(conv_hi, 1)

        def act_gate(n):
            nc.scalar.wait_ge(gate_arg, n)
            nc.scalar.activation(gate_e[:, :, :], gate_e[:, :, :], ACT.Exp).then_inc(gate_exp, 1)

        def act_values(e, i):
            u = USE["v", e, i]
            nc.scalar.wait_ge(group_done, u + 1)
            nc.scalar.activation(vs[0][:, i, :], bank(6 + u % 2, T, HD), ACT.Copy).then_inc(group_hi, 1)

        def act_exp(e, i):
            nc.scalar.wait_ge(max_ready, e * NT + i + 1)
            r = i % 2
            nc.scalar.activation(pexp[0:T, 0:seen(i)], PS[0:T, 0:3, :].rearrange("p b c -> p (b c)")[:, 0:seen(i)], ACT.Exp,
                                 bias=att_max[:, 2 + r:3 + r], scale=SCALE, accum_out=att_den[:, r:r + 1]).then_inc(pexp_ready, 1)

        def act_turned(e, i):
            nc.scalar.wait_ge(pexp_turned, e * NT + i + 1)
            nc.scalar.activation(pT[0][:, 0:i + 1, :], blocks(3, NT)[0:T, 0:i + 1, 0:T], ACT.Copy).then_inc(pexp_hi, 1)

        def scale(i):
            batch = [i in b for b in Y_LOADS].index(True)
            nc.scalar.wait_ge(y_loaded[batch], 32)
            for e in range(HEADS):
                part = y_in[:, i, e * HD:(e + 1) * HD]
                last = nc.scalar.activation(part, part, ACT.Copy, scale=gate_scale[:, e, i:i + 1])
            last.then_inc(y_scaled, 1)

        def last_high(i):
            nc.scalar.wait_ge(y_turned, i + 1)
            if i >= 2:
                nc.scalar.wait_ge(proj_done, i - 1)
            nc.scalar.activation(yT[0][:, i % 2, :, :], blocks(2 * (i % 2), KC)[:, :, 0:T], ACT.Copy).then_inc(yt_hi, 1)

        def act_ffn(act):
            act_rows_high(1, NT - 1)
            for b in range(1, 3):
                act_weight(b)
            act.wait_ge(tabs_in, TABS)
            for e in range(HEADS):
                for n in range(HC * 3):
                    act_column_group("k", e, n)
                    if e == 0 and n in (1, 3):
                        act_conv_high(n // 2)
                    if e == 1 and n in (1, 3):
                        act_gate(n // 2 + 1)
                act_values(e, 0)
                act_exp(e, 0)
                for i in range(NT):
                    if (e, i) == (HEADS - 1, NT - 1):
                        act.wait_ge(gate_ready, 1)
                        scale(0)
                    act_turned(e, i)
                    if i + 1 < NT:
                        act_exp(e, i + 1)
                        act_values(e, i + 1)
                    elif e + 1 < HEADS:
                        act_columns("q", e + 1)
                    else:
                        last_high(0)
                    if i in (2, 5, NT - 2):
                        act_weight(3 * e + 3 + (2, 5, NT - 2).index(i))

        def dve_column_group(kind, e, n):
            to = qT if kind == "q" else kT
            c, start, size = column_group(n)
            u = USE[kind, e, n]
            nc.vector.wait_ge(group_hi, HIGH[kind, e, n] + 1)
            nc.vector.scalar_tensor_tensor(to[1][:, c, start:start + size], bank(6 + u % 2, P, size), bias_col(kind, e, c),
                                           to[0][:, c, start:start + size].bitcast(F32), ALU.add, ALU.subtract).then_inc(group_free, 1)

        def dve_columns(kind, e):
            for n in range(HC * 3):
                dve_column_group(kind, e, n)

        def dve_first_queries(own):
            dve = nc.vector
            own.mark(dve.memset(q_raw[:, :, 0:1], 0.0))
            own.mark(dve.memset(q_raw[:, :, N + 1:N + 2], 0.0))

            def queries(groups):
                for n in groups:
                    c, start, size = column_group(n)
                    u = USE["q", 0, n]
                    dve.wait_ge(group_done, u + 1)
                    dve.tensor_scalar(q_raw[:, c, 1 + start:1 + start + size], bank(6 + u % 2, P, size), bias_col("q", 0, c), None, ALU.add).then_inc(group_free, 1)

            queries(range(0, HC))
            dve_rows_low(1, NT - 1)
            queries(range(HC, 3 * HC))
            own.wait()
            dve.wait_ge(group_free, 3 * HC)

        def conv_tap(c, tap, own):
            dve, x_ = nc.vector, q_raw[:, c, tap:tap + N]
            if tap == 1:
                own.done(dve.tensor_scalar(pexp[:, :], x_, conv_wc[:, c, 1:2], conv_bc[:, c:c + 1], ALU.mult, ALU.add))
            elif tap == 0:
                own.done(dve.scalar_tensor_tensor(pexp[:, :], x_, conv_wc[:, c, 0:1], pexp[:, :], ALU.mult, ALU.add))
            else:
                dve.scalar_tensor_tensor(pexp[:, :], x_, conv_wc[:, c, 2:3], pexp[:, :], ALU.mult, ALU.add).then_inc(conv_ready, 1)

        def conv_low(c, own):
            nc.vector.wait_ge(conv_hi, c + 1)
            own.done(nc.vector.tensor_tensor(qT[1][:, c, :], pexp[:, :], qT[0][:, c, :].bitcast(F32), ALU.subtract))

        def dve_first_keys(own):
            conv_tap(0, 1, own)
            conv_tap(0, 0, own)
            dve_column_group("k", 0, 0)
            conv_tap(0, 2, own)
            dve_column_group("k", 0, 1)
            conv_low(0, own)
            conv_tap(1, 1, own)
            dve_column_group("k", 0, 2)
            conv_tap(1, 0, own)
            conv_tap(1, 2, own)
            dve_column_group("k", 0, 3)
            conv_low(1, own)
            dve_column_group("k", 0, 4)
            dve_column_group("k", 0, 5)

        def dve_second_keys(own):
            dve_column_group("k", 1, 0)
            gate_logits(own)
            dve_column_group("k", 1, 1)
            gate_kept(own)
            dve_column_group("k", 1, 2)
            dve_column_group("k", 1, 3)
            gate_weights(own)
            dve_column_group("k", 1, 4)
            dve_column_group("k", 1, 5)

        def dve_values(e, i):
            u = USE["v", e, i]
            nc.vector.wait_ge(group_hi, HIGH["v", e, i] + 1)
            if e == 0:
                nc.vector.tensor_tensor(gate_h[:, i, :], PS[0:T, 6 + u % 2, HD:WG], bg1_b[:, :], ALU.add)
            nc.vector.tensor_tensor(vs[1][:, i, :], bank(6 + u % 2, T, HD), vs[0][:, i, :].bitcast(F32), ALU.subtract).then_inc(group_free, 1)

        def dve_max(e, i, own):
            dve, r = nc.vector, i % 2
            s = PS[0:T, 0:3, :].rearrange("p b c -> p (b c)")
            dve.wait_ge(scores_done, e * NT + i + 1)
            own.done(dve.tensor_tensor(s[:, i * T:seen(i)], s[:, i * T:seen(i)], tri[:, :], ALU.add))
            own.done(dve.tensor_reduce(att_max[:, r:r + 1], s[:, 0:seen(i)], AX.X, ALU.max))
            dve.tensor_scalar(att_max[:, 2 + r:3 + r], att_max[:, r:r + 1], -SCALE, None, ALU.mult).then_inc(max_ready, 1)

        def dve_turned(e, i):
            nc.vector.wait_ge(pexp_hi, e * NT + i + 1)
            nc.vector.tensor_tensor(pT[1][:, 0:i + 1, :], blocks(3, NT)[0:T, 0:i + 1, 0:T], pT[0][:, 0:i + 1, :].bitcast(F32), ALU.subtract).then_inc(pexp_lo, 1)

        def dve_weighted(e, i, own):
            dve, r, u, m = nc.vector, i % 2, USE["y", e, i], e * NT + i
            own.done(dve.reciprocal(att_den[:, 2 + r:3 + r], att_den[:, r:r + 1]))
            dve.wait_ge(group_done, u + 1)
            if m >= 2:
                dve.wait_ge(ys_stored[m % 2], 32 * (m // 2))
            dve.scalar_tensor_tensor(ys_out[:, m % 2, :], bank(6 + u % 2, T, HD), att_den[:, 2 + r:3 + r],
                                     bv_b[:, e * HD:(e + 1) * HD], ALU.mult, ALU.add).then_inc(group_free, 1)

        def gate_less_max(own):
            dve = nc.vector
            own.done(dve.tensor_tensor(gate_c[:, 0, :], gate_e[:, 0, :], gate_e[:, 1, :], ALU.max))
            own.done(dve.tensor_tensor(gate_c[:, 0, :], gate_c[:, 0, :], gate_e[:, 2, :], ALU.max))
            dve.tensor_tensor(gate_e[:, :, :], gate_e[:, :, :], gate_c[:, 0:1, :].to_broadcast([T, HEADS, NT]), ALU.subtract).then_inc(gate_arg, 1)

        def gate_over_sum(to, own):
            dve = nc.vector
            own.done(dve.tensor_tensor(gate_c[:, 0, :], gate_e[:, 0, :], gate_e[:, 1, :], ALU.add))
            own.done(dve.tensor_tensor(gate_c[:, 0, :], gate_c[:, 0, :], gate_e[:, 2, :], ALU.add))
            own.done(dve.reciprocal(gate_c[:, 0, :], gate_c[:, 0, :]))
            return dve.tensor_tensor(to[:, :, :], gate_e[:, :, :], gate_c[:, 0:1, :].to_broadcast([T, HEADS, NT]), ALU.mult)

        def gate_logits(own):
            dve = nc.vector
            flat = gate_h[:, :, :].rearrange("p a b -> p (a b)")
            own.done(dve.tensor_scalar(flat, flat, 0.0, None, ALU.max))
            for e in range(HEADS):
                own.done(dve.tensor_tensor(gate_t[:, :, :], gate_h[:, :, :], wg2_b[:, :, e:e + 1].rearrange("p a b -> p b a").to_broadcast([T, NT, GATE]), ALU.mult))
                own.done(dve.tensor_reduce(gate_e[:, e, :], gate_t[:, :, :], AX.X, ALU.add))
                own.done(dve.tensor_scalar(gate_e[:, e, :], gate_e[:, e, :], bg2_b[:, e:e + 1], None, ALU.add))
            gate_less_max(own)

        def gate_kept(own):
            dve = nc.vector
            dve.wait_ge(gate_exp, 1)
            own.done(gate_over_sum(gate_e, own))
            g = [gate_e[:, e, :] for e in range(HEADS)]
            tests = (((0, 1, ALU.is_lt), (0, 2, ALU.is_lt)), ((1, 0, ALU.is_le), (1, 2, ALU.is_lt)), ((2, 0, ALU.is_le), (2, 1, ALU.is_le)))
            for e, pair in enumerate(tests):
                for n, (a_, b_, op) in enumerate(pair):
                    own.mark(dve.tensor_tensor(gate_c[:, 1 + n, :], g[a_], g[b_], op))
                own.wait()
                own.done(dve.tensor_tensor(gate_c[:, 3, :], gate_c[:, 1, :], gate_c[:, 2, :], ALU.mult))
                own.done(dve.tensor_scalar(gate_scale[:, e, :], gate_c[:, 3, :], -1.0, 1.0, ALU.mult, ALU.add))
            gate_less_max(own)

        def gate_weights(own):
            dve = nc.vector
            dve.wait_ge(gate_exp, 2)
            own.done(dve.tensor_tensor(gate_e[:, :, :], gate_e[:, :, :], gate_scale[:, :, :], ALU.mult))
            gate_over_sum(gate_scale, own).then_inc(gate_ready, 1)

        def x2_rows(i):
            return x2_in[:, i, :] if i < NT - 1 else x2_last[:, :]

        def turned_low(i):
            nc.vector.wait_ge(yt_hi, i + 1)
            nc.vector.tensor_tensor(yT[1][:, i % 2, :, :], blocks(2 * (i % 2), KC)[:, :, 0:T], yT[0][:, i % 2, :, :].bitcast(F32), ALU.subtract).then_inc(yt_lo, 1)

        def dve_ffn(dve, own):
            dve.wait_ge(tabs_in, TABS)
            dve_first_queries(own)
            dve.wait_ge(tri_ready, 2)
            for e in range(HEADS):
                if e == 0:
                    dve_first_keys(own)
                elif e == 1:
                    dve_second_keys(own)
                else:
                    dve_columns("k", e)
                dve_values(e, 0)
                dve_max(e, 0, own)
                for i in range(NT):
                    dve_turned(e, i)
                    if i + 1 < NT:
                        dve_max(e, i + 1, own)
                        dve_values(e, i + 1)
                    elif e + 1 < HEADS:
                        dve_columns("q", e + 1)
                    else:
                        turned_low(0)
                    dve_weighted(e, i, own)

        def pool_ffn(pool):
            pool.wait_ge(LAYER[1]["probs_ready"], NT)
            pool.memset(tri[:, :], 0.0).then_inc(tri_ready, 1)
            pool.wait_ge(tri_ready, 1)
            pool.affine_select(out=tri[:, :], in_=tri[:, :], compare_op=ALU.is_ge, fill=FAR,
                               base=0, pattern=[[-1, T]], channel_multiplier=1).then_inc(tri_ready, 1)
            for b in range(1, BLOCKS + HEADS):
                pool_weight(pool, b)

        def pool_weight(pool, b):
            width = WG if b == 2 else WB
            pool.wait_ge(ws_hi, b + 1)
            pool.tensor_tensor(Ws[1][b % 3][:, :, 0:width], w_raw[:, :, 0:width], Ws[0][b % 3][:, :, 0:width].bitcast(F32), ALU.subtract).then_inc(ws_lo, 1)

        TABS = 16 * 7

        def sp_ffn(sp):
            L = LAYER[1]
            sp.wait_ge(L["probs_ready"], NT)
            with nc.allow_non_contiguous_dma(reason="small tables, a column for each chunk"):
                sp.dma_start(bqk_c[:, :], ffn["bqk"].rearrange("(c p) -> p c", p=P)).then_inc(tabs_in, 16)
                sp.dma_start(conv_wc[:, :, :], ffn["conv_w"].rearrange("(c p) o k -> p c (o k)", p=P)).then_inc(tabs_in, 16)
                sp.dma_start(conv_bc[:, :], ffn["conv_b"].rearrange("(c p) -> p c", p=P)).then_inc(tabs_in, 16)
            for to, frm in ((bg1_b, ffn["bg1"]), (bg2_b, ffn["bg2"])):
                sp.dma_start(to[:, :], frm.rearrange("(o n) -> o n", o=1).to_broadcast([T, frm.shape[0]])).then_inc(tabs_in, 16)
            sp.dma_start(wg2_b[:, :, :].rearrange("p a b -> p (a b)"), ffn["Wg2"].rearrange("(o a) b -> o (a b)", o=1).to_broadcast([T, GATE * HEADS])).then_inc(tabs_in, 16)
            sp.dma_start(bv_b[:, :], ffn["bv"].rearrange("(o a) b -> o (a b)", o=1).to_broadcast([T, D])).then_inc(tabs_in, 16)

        @block.sync
        def _(sp):
            sp.dma_start(dst_i[:, :], dst.rearrange("(g e) -> g e", g=G)).then_inc(edges_in, 16)
            sp.dma_start(src_i[:, :], src.rearrange("(g e) -> g e", g=G)).then_inc(edges_in, 16)
            with nc.allow_non_contiguous_dma(reason="the first destination of each group"):
                sp.dma_start(bases[:, LAG:LAG + G], dst.rearrange("(o g e) -> o g e", g=G, o=1)[:, :, 0]).then_inc(bases_in, 16)
            xr = x.rearrange("(t p) d -> p t d", p=T)
            rows_in(sp, xall[:, 0:2, :], xr[:, 0:2, :], x_head_in)
            for c in range(KC):
                sp.dma_start(Wraw[:, c, 0:D], gnn[0]["W"][c * P:(c + 1) * P, :]).then_inc(w_in, 16)
            rows_in(sp, xall[:, 2:NT, :], xr[:, 2:NT, :], x_in)
            sp.wait_ge(xn_ready, NT)
            for a, name in enumerate(("as", "ad")):
                sp.dma_start(attb2[:, a, :], gnn[1][name].rearrange("(o n) -> o n", o=1).to_broadcast([P, D])).then_inc(att2_in, 16)
            for c in list(range(2, KC)) + [0, 1]:
                if c == 0:
                    sp.wait_ge(early_turned, 2 * EARLY + 1)
                sp.dma_start(Wraw2[:, c, 0:D], gnn[1]["W"][c * P:(c + 1) * P, :]).then_inc(w2_in, 16)
            sp.wait_ge(counts_ready, NT - EARLY)
            sp.dma_start(bias_b[:, :], gnn[0]["b"].rearrange("(o n) -> o n", o=1).to_broadcast([T, D])).then_inc(LAYER[0]["bias_in"], 16)
            sp.wait_ge(LAYER[0]["rows_out"], 2 * NT)
            sp.dma_start(bias_b[:, :], gnn[1]["b"].rearrange("(o n) -> o n", o=1).to_broadcast([T, D])).then_inc(LAYER[1]["bias_in"], 16)
            sp.wait_ge(split_hi, NT)
            sp.wait_ge(split_dve, NT // 2)
            sp.wait_ge(split_pool, NT // 2)
            x2r = x2_dram.rearrange("(t p) d -> t p d", p=T)
            xt = x.rearrange("(t p) d -> t p d", p=T)
            def weight_in(b):
                if b:
                    sp.wait_ge(ws_lo, b)
                if b < BLOCKS and b % 3 < 2:
                    col = (b % 3) * D + (b // 3) * HD
                    frm = ffn["Wqk"][:, col:col + WB]
                elif b < BLOCKS:
                    frm = ffn["Wv"][b // 3]
                else:
                    frm = ffn["Wp"][:, (b - BLOCKS) * WB:(b - BLOCKS + 1) * WB]
                sp.dma_start(w_raw[:, :, 0:WB], frm.rearrange("(k p) n -> p k n", p=P)).then_inc(ws_in, 16)
                if b == 2:
                    sp.dma_start(w_raw[:, :, WB:WG], ffn["Wg1"].rearrange("(k p) n -> p k n", p=P)).then_inc(ws_in, 16)

            rows_in(sp, x_plus, xt[0], x_again)
            weight_in(0)
            for d in range(NT):
                sp.wait_ge(LAYER[1]["rows_out"], 2 * d + 2)
                rows_out_to(sp, x2r[d], rows, x2_stored)
                if d + 1 < NT:
                    rows_in(sp, x_plus, xt[d + 1], x_again)
                if d == NT - 2:
                    sp_ffn(sp)
            sp.wait_ge(x2_stored, 32 * NT)
            for b in range(1, 4):
                weight_in(b)
            yr = y_dram.rearrange("(t p) d -> t p d", p=T)

            def y_back(n):
                tiles = Y_LOADS[n]
                m = (HEADS - 1) * NT + tiles[-1]
                for k in (m - 1, m):
                    sp.wait_ge(ys_stored[k % 2], 32 * (k // 2 + 1))
                rows_in(sp, y_in[:, tiles[0]:tiles[-1] + 1, :], y_dram.rearrange("(t p) d -> p t d", p=T)[:, tiles[0]:tiles[-1] + 1, :], y_loaded[n])

            for m in range(HEADS * NT):
                e, i = m // NT, m % NT
                sp.wait_ge(group_free, USE["y", e, i] + 1)
                rows_out_to(sp, yr[i][:, e * HD:(e + 1) * HD], ys_out[:, m % 2, :], ys_stored[m % 2])
                if i in (2, 5, NT - 2) and m < HEADS * NT - 2:
                    weight_in(3 * e + 4 + (2, 5, NT - 2).index(i))
                if m == 0:
                    sp.wait_ge(conv_ready, HC)
                    sp.dma_start(bp_b[:, :], ffn["bp"].rearrange("(o n) -> o n", o=1).to_broadcast([T, D])).then_inc(bp_in, 16)
                if m == HEADS * NT - 3:
                    sp.wait_ge(group_done, USE["v", HEADS - 1, NT - 1] + 1)
                    y_back(0)
                    y_back(1)
                    rows_in(sp, x2_in, x2_dram.rearrange("(t p) d -> p t d", p=T)[:, 0:NT - 1, :], x2_loaded[0])
            y_back(2)
            y_back(3)
            sp.wait_ge(pexp_ready, HEADS * NT)
            rows_in(sp, x2_last, x2_dram[(NT - 1) * T:N, :], x2_loaded[1])
            y_back(4)
            outr = out.rearrange("(t p) d -> t p d", p=T)
            for i in range(NT):
                sp.wait_ge(out_ready, i + 1)
                rows_out_to(sp, outr[i], out_sb[:, i % 2, :], out_stored[i % 2])
            for p in range(2):
                sp.wait_ge(out_stored[p], 32 * NT // 2)

        def turned_rows_low(pool, n):
            pool.wait_ge(xt_hi_ready, n)
            pool.wait_ge(xt_raw_ready, n)
            pool.tensor_tensor(XT[1][:, :, :], xt_raw[:, :, :], XT[0][:, :, :].bitcast(F32), ALU.subtract).then_inc(xt_lo_ready, 1)

        def messages_low(pool, i, n):
            pool.wait_ge(h_hi_ready, n)
            pool.tensor_tensor(H[1][:, bass.ds(i, 1), :].rearrange("p a d -> p (a d)"), h_raw[:, 0:D],
                               H[0][:, bass.ds(i, 1), :].rearrange("p a d -> p (a d)").bitcast(F32), ALU.subtract).then_inc(h_lo_ready, 1)

        @block.gpsimd
        def _(pool):
            own = Own(pool, pool_own)
            own.mark(pool.memset(ident[:, :], 0.0))
            pool.memset(ones[:, :], 1.0).then_inc(consts_ready, 1)
            pool.memset(minus_half[:, :], -0.5).then_inc(h_free, 2)
            own.mark(pool.memset(eps[:, :], LN_EPS))
            own.done(pool.iota(iota_i[:, :], pattern=[[1, NT * W]], base=0, channel_multiplier=0))
            own.done(pool.iota(place_i[:, :], pattern=[[1, 1]], base=0, channel_multiplier=T))
            own.mark(pool.tensor_copy(place[:, :], place_i[:, :]))
            pool.tensor_copy(iota[:, :], iota_i[:, :]).then_inc(consts_ready, 1)
            pool.affine_select(out=ident[:, :], in_=ident[:, :], compare_op=ALU.not_equal, fill=1.0,
                               base=0, pattern=[[-1, P]], channel_multiplier=1).then_inc(consts_ready, 1)
            own.done(pool.memset(countsT[:, :, :].rearrange("p a b -> p (a b)").bitcast(mybir.dt.uint32), 0))
            pool.wait_ge(consts_ready, 3)
            for t in range(NT):
                last = pool.tensor_copy(countsT[:, t, t * T:(t + 1) * T], ident[0:T, 0:T])
            last.then_inc(countsT_filled, 1)
            pool.wait_ge(consts_ready, 3)
            pool.wait_ge(stats_ready, 1)
            own.done(pool.tensor_tensor(rstd[:, 0:2], varep[:, 0:2], minus_half[:, 0:2], ALU.pow))
            pool.tensor_tensor(shift[:, 0:2], negmean[:, 0:2], rstd[:, 0:2], ALU.mult).then_inc(rstd_ready, 1)
            pool.wait_ge(w_hi_ready, 1)
            pool.tensor_tensor(Wg[1][:, :, 0:D], Wraw[:, :, 0:D], Wg[0][:, :, 0:D].bitcast(F32), ALU.subtract).then_inc(w_lo_ready, 1)
            pool.wait_ge(att_hi_ready, 1)
            pool.tensor_tensor(Wg[1][:, :, D:WX], Wraw[:, :, D:WX], Wg[0][:, :, D:WX].bitcast(F32), ALU.subtract).then_inc(w_lo_ready, 1)
            pool.wait_ge(sums_ready, 1)
            own.mark(pool.tensor_scalar(negmean[:, 2:NT], sums[:, 2:NT], -1.0 / D, None, ALU.mult))
            pool.tensor_scalar(mean_root[:, 2:NT], sums[:, 2:NT], -D ** -1.5, None, ALU.mult).then_inc(means_ready, 1)
            def next_scale(i):
                at = bass.ds(i, 1)
                pool.wait_ge(squares_ready, i - 1)
                own.done(pool.tensor_tensor(varep[:, at], sums[:, at], eps[:, :], ALU.add))
                own.done(pool.tensor_tensor(rstd[:, at], varep[:, at], minus_half[:, 0:1], ALU.pow))
                pool.tensor_tensor(shift[:, at], negmean[:, at], rstd[:, at], ALU.mult).then_inc(rstd_ready, 1)

            turned_rows_low(pool, 1)
            next_scale(2)
            with pool.Fori(1, NT - 2) as i:
                kept = own.enter(i - 1, 2)
                turned_rows_low(pool, i + 1)
                messages_low(pool, i - 1, i)
                next_scale(i + 2)
                own.leave(kept, NT - 3)
            for i in (NT - 2, NT - 1):
                turned_rows_low(pool, i + 1)
                messages_low(pool, i - 1, i)
            messages_low(pool, NT - 1, NT)
            pool.wait_ge(w2_in, 16 * KC)
            pool.wait_ge(att2_in, 32)
            for n in range(ACT_COLUMNS):
                if n >= 2:
                    pool.wait_ge(att2_act, n - 1)
                pool.tensor_tensor(product[:, n % 2, :], Wraw2[:, n // 2, 0:D], attb2[:, n % 2, :], ALU.mult).then_inc(product_ready, 1)
            for h in range(2):
                half = slice(h * KC // 2, (h + 1) * KC // 2)
                pool.wait_ge(w2_hi, h + 1)
                pool.tensor_tensor(Wg[1][:, half, :], Wraw2[:, half, :], Wg[0][:, half, :].bitcast(F32), ALU.subtract).then_inc(w2_lo, 1)
            for s in range(1, NT, 2):
                pool.wait_ge(split_hi, s + 1)
                pool.tensor_tensor(H[1][:, s, :], h_next[:, s, :], H[0][:, s, :].bitcast(F32), ALU.subtract).then_inc(split_pool, 1)
            L = LAYER[1]
            pool.wait_ge(split_dve, NT // 2)
            pool.wait_ge(split_pool, NT // 2)
            pool.memset(half2[:, :], -0.5).then_inc(half_ready, 1)
            pool.wait_ge(L["bias_in"], 16)
            pool.wait_ge(half_ready, 1)

            def add_bias(d):
                pool.wait_ge(x_again, 32 * (d + 1))
                pool.tensor_tensor(x_plus[:, :], x_plus[:, :], bias_b[:, :], ALU.add).then_inc(x_plus_ready, 1)

            add_bias(0)
            for d in range(NT):
                if d + 1 < NT:
                    add_bias(d + 1)
                pool.wait_ge(var_ready, d + 1)
                own.done(pool.tensor_tensor(ln2[:, 2:3], ln2[:, 1:2], half2[:, :], ALU.pow))
                pool.tensor_tensor(ln2[:, 3:4], ln2[:, 0:1], ln2[:, 2:3], ALU.mult).then_inc(ln_ready, 1)
                if d == NT // 2:
                    pool_weight(pool, 0)
            pool_ffn(pool)
            pool.wait_ge(bp_in, 16)
            for i in range(NT):
                pool.wait_ge(x2_loaded[i // (NT - 1)], 32)
                pool.tensor_tensor(x2_rows(i), x2_rows(i), bp_b[:, :], ALU.add).then_inc(x2_plus, 1)

        def normalise(i):
            nc.scalar.wait_ge(rstd_ready, i if not isinstance(i, int) or i >= 2 else 1)
            nc.scalar.activation(xn[:, :], xall[:, bass.ds(i, 1), :].rearrange("p a d -> p (a d)"), ACT.Identity,
                                 bias=shift[:, bass.ds(i, 1)], scale=rstd[:, bass.ds(i, 1)]).then_inc(xn_ready, 1)

        def squares(i):
            at = bass.ds(i, 1)
            if not isinstance(i, int):
                nc.scalar.wait_ge(squares_ready, i - 2)
            nc.scalar.activation(junk_x[0:T, :], xall[:, at, :].rearrange("p a d -> p (a d)"), ACT.Square, bias=mean_root[:, at], scale=D ** -0.5,
                                 accum_out=sums[:, at]).then_inc(squares_ready, 1)

        def act_rows(i):
            peeled = isinstance(i, int)
            nc.scalar.wait_ge(xn_turned, i + 1)
            if not peeled or i >= 1:
                nc.scalar.wait_ge(h_done, 2 * i)
            nc.scalar.activation(XT[0][:, :, :], blocks(0, KC)[:, :, 0:T], ACT.Copy).then_inc(xt_hi_ready, 1)
            if not peeled or i >= 1:
                act_second_half(i - 1)
                nc.scalar.wait_ge(xt_lo_ready, i)
            nc.scalar.activation(xt_raw[:, :, :], blocks(0, KC)[:, :, 0:T], ACT.Copy).then_inc(xt_raw_ready, 1)

        def message_tile(i):
            return H[0][:, bass.ds(i, 1), :].rearrange("p a d -> p (a d)")

        def act_first_half(i):
            nc.scalar.wait_ge(h_done, 2 * i + 1)
            if not isinstance(i, int) or i >= 1:
                nc.scalar.wait_ge(h_lo_ready, i)
            nc.scalar.activation(h_raw[:, 0:HALF], bank(5, T, HALF), ACT.Copy)
            nc.scalar.activation(message_tile(i)[:, 0:HALF], bank(5, T, HALF), ACT.Copy).then_inc(h_free, 1)

        def act_early_columns(d):
            nc.scalar.wait_ge(window_free, (d + 2) * PER_TILE + LAG)
            nc.scalar.wait_ge(early_turned, 2 * d + 1)
            nc.scalar.activation(ct_early[:, :, :], countsT[:, :, bass.ds(d * T, T)], ACT.Copy).then_inc(early_conv, 1)

        def act_early_counts(d, h):
            nc.scalar.wait_ge(early_turned, 2 * d + 2 + h)
            to = counts[:, bass.ds(d, 1), h * N // 2:(h + 1) * N // 2].rearrange("p o (a b) -> p (o a) b", b=T)
            nc.scalar.activation(to, blocks(3, NT // 2)[0:T, :, 0:T], ACT.Copy).then_inc(early_put, 1)

        def act_second_half(i):
            nc.scalar.wait_ge(h_done, 2 * i + 2)
            nc.scalar.activation(h_raw[:, HALF:WX], bank(6, T, WX - HALF), ACT.Copy)
            nc.scalar.activation(message_tile(i)[:, HALF:D], bank(6, T, HALF), ACT.Copy).then_inc(h_hi_ready, 1)
            nc.scalar.activation(asd[:, bass.ds(i, 1), :].rearrange("p a b -> p (a b)"), PS[0:T, 6, HALF:HALF + 2], ACT.Copy).then_inc(h_free, 1)

        @block.scalar
        def _(act):
            act.dma_start(attb[:, 0, :], gnn[0]["as"].rearrange("(o n) -> o n", o=1).to_broadcast([P, D])).then_inc(att_in, 16)
            act.dma_start(attb[:, 1, :], gnn[0]["ad"].rearrange("(o n) -> o n", o=1).to_broadcast([P, D])).then_inc(att_in, 16)
            act.wait_ge(edge_rows_turned, 1)
            for b, t in ((0, tab_low), (1, tab_win)):
                for c in range(2):
                    act.activation(t[:, :, :, c].rearrange("p g t -> p t g"), bank(b, T, ET * G).rearrange("p (t g) -> p t g", t=ET), ACT.Copy)
            for b, t in ((2, tab_dst), (3, tab_high)):
                act.activation(t[:, :, :].rearrange("p a b -> p (a b)"), bank(b, T, ET * G), ACT.Copy)
            act.activation(flag[:, :], bank(4, 1, 1), ACT.Copy).then_inc(tables_ready, 1)
            act.wait_ge(w_in, 16 * KC)
            act.activation(Wg[0][:, :, 0:D], Wraw[:, :, 0:D], ACT.Copy).then_inc(w_hi_ready, 1)
            normalise(0)
            act_rows(0)
            normalise(1)
            act.wait_ge(att_cols_ready, 1)
            act.activation(Wg[0][:, :, D:WX], Wraw[:, :, D:WX], ACT.Copy).then_inc(att_hi_ready, 1)
            act.wait_ge(x_in, 32)
            for i in range(2, NT):
                last = act.activation(xall[:, i, :], xall[:, i, :], ACT.Copy, accum_out=sums[:, i:i + 1])
            last.then_inc(sums_ready, 1)
            act.wait_ge(means_ready, 1)
            squares(2)
            act_first_half(0)
            act_rows(1)
            normalise(2)
            squares(3)
            act_first_half(1)
            act_rows(2)
            normalise(3)
            squares(4)
            act_early_columns(0)
            act_first_half(2)
            with act.Fori(3, NT - 2) as i:
                act_rows(i)
                act_early_counts(i - 3, 0)
                normalise(i + 1)
                squares(i + 2)
                act_first_half(i)
                act_early_counts(i - 3, 1)
                act_early_columns(i - 2)
            for i in (NT - 2, NT - 1):
                act_rows(i)
                act_early_counts(i - 3, 0)
                if i + 1 < NT:
                    normalise(i + 1)
                act_first_half(i)
                act_early_counts(i - 3, 1)
                if i + 1 < NT:
                    act_early_columns(i - 2)
            act_second_half(NT - 1)
            act.wait_ge(countsT_ready, 1)
            for d in range(EARLY, NT):
                if d >= EARLY + 2:
                    act.wait_ge(ct_turned, d - EARLY - 1)
                act.activation(ct_f[:, d % 2, :, :], countsT[:, :, d * T:(d + 1) * T], ACT.Copy).then_inc(ct_conv, 1)
                if d == EARLY:
                    act_terms(0)
                    act_first_line(0)
            act_exp_edges(0, 0)
            act_column(0)
            act_column(1)
            act_attention(0)
            act_attention(1)
            act_ffn(act)

            for i in range(1, NT):
                scale(i)
                last_high(i)

        def onehots(g, buf):
            for hot, n, tab in ((oh_src, OHS, tab_low), (oh_win, NT * W, tab_win)):
                last = nc.vector.tensor_tensor(hot[:, buf, :, :].rearrange("p t (n c) -> p t n c", c=2),
                                               iota[:, 0:n].rearrange("p (o n c) -> p o n c", o=1, c=2).to_broadcast([T, ET, n // 2, 2]),
                                               tab[:, bass.ds(g, 1), :, :].rearrange("p g t (o c) -> p (g t) o c", o=1).to_broadcast([T, ET, n // 2, 2]), ALU.is_equal)
            last.then_inc(onehots_ready, 1)

        def add_window(dve, q, buf, start):
            dve.wait_ge(group_counted, q + LAG)
            cols = countsT[:, :, bass.ds(start, W)]
            nc.vector.tensor_tensor(cols, bank(WINDOW_BANKS[buf % 2], T, NT * W).rearrange("p (a b) -> p a b", a=NT), cols, ALU.add).then_inc(window_free, 1)

        def put_counts(dve, d):
            dve.wait_ge(ct_turned, d - EARLY + 1)
            nc.vector.tensor_copy(counts[:, d, :].rearrange("p (a b) -> p a b", a=NT), blocks(3 * (d % 2), NT)[0:T, :, 0:T]).then_inc(counts_ready, 1)

        @block.vector
        def _(dve):
            own = Own(dve, dve_own)
            nc.vector.memset(small[:, 0:1], 0.0).then_inc(window_free, LAG)
            nc.vector.memset(small[:, 7:8], 0.0).then_inc(group_counted, LAG - 1)
            nc.vector.memset(stat[:, 0:1], 0.0).then_inc(onehots_ready, 1)
            nc.vector.memset(stat[:, 1:2], 0.0).then_inc(early_turned, 1)
            nc.vector.memset(stat[:, 2:3], 0.0).then_inc(early_put, 1)
            dve.wait_ge(edges_in, 32)
            own.mark(nc.vector.tensor_copy(dst_f[:, :], dst_i[:, :]))
            own.done(nc.vector.tensor_scalar(src_high[:, :], src_i[:, :], -(T - 1) / 2, 1.0 / T, ALU.add, ALU.mult))
            own.done(nc.vector.tensor_scalar(src_high[:, :], src_high[:, :], ROUND, ROUND, ALU.add, ALU.subtract))
            own.mark(nc.vector.scalar_tensor_tensor(src_low[:, :], src_high[:, :], -float(T), src_i[:, :], ALU.mult, ALU.add))
            own.done(nc.vector.tensor_scalar(rel[:, :], dst_f[:, :], dst_f[:, 0:1], None, ALU.subtract))
            own.mark(nc.vector.scalar_tensor_tensor(win[:, :], src_high[:, :], float(W), rel[:, :], ALU.mult, ALU.add))
            own.mark(nc.vector.tensor_reduce(small[0:G, 1:2], rel[:, :], AX.X, ALU.max))
            own.done(nc.vector.tensor_reduce(small[0:G, 2:3], rel[:, :], AX.X, ALU.min))
            own.done(nc.vector.tensor_scalar(small[0:G, 3:4], small[0:G, 1:2], float(W - 1), None, ALU.is_gt))
            own.mark(nc.vector.scalar_tensor_tensor(small[0:G, 4:5], small[0:G, 2:3], 0.0, small[0:G, 3:4], ALU.is_lt, ALU.add))
            dve.wait_ge(consts_ready, 2)
            own.done(nc.vector.tensor_scalar(small[0:G, 5:6], dst_f[:, 0:1], float(PER_TILE), float(PER_TILE * T), ALU.mult, ALU.add))
            own.done(nc.vector.tensor_tensor(small[0:G, 6:7], small[0:G, 5:6], place[:, :], ALU.is_lt))
            nc.vector.tensor_tensor(small[0:G, 4:5], small[0:G, 4:5], small[0:G, 6:7], ALU.add).then_inc(edge_rows_ready, 1)
            dve.wait_ge(x_head_in, 32)
            for i in range(2):
                for h in range(2):
                    last = nc.vector.bn_stats(bn[:, i, h, :], xall[:, i, h * HALF:(h + 1) * HALF])
            own.done(last)
            for i in range(2):
                last = nc.vector.bn_aggr(mv[:, i, :], bn[:, i, :, :])
            own.done(last)
            own.mark(nc.vector.tensor_scalar(negmean[:, 0:2], mv[:, :, 0], -1.0, None, ALU.mult))
            nc.vector.tensor_scalar(varep[:, 0:2], mv[:, :, 1], LN_EPS, None, ALU.add).then_inc(stats_ready, 1)
            dve.wait_ge(w_in, 16 * KC)
            dve.wait_ge(att_in, 32)
            for c in range(KC):
                for a in range(2):
                    own.done(nc.vector.tensor_tensor_reduce(out=junk_w[:, :], in0=Wraw[:, c, 0:D], in1=attb[:, a, :], scale=1.0, scalar=0.0,
                                                            op0=ALU.mult, op1=ALU.add, accum_out=Wraw[:, c, D + a:D + a + 1]))
            nc.vector.memset(small[:, 5:6], 0.0).then_inc(att_cols_ready, 1)
            dve.wait_ge(consts_ready, 3)
            dve.wait_ge(countsT_filled, 1)
            dve.wait_ge(tables_ready, 1)
            dve.wait_ge(bases_in, 16)
            spread = dve.value_load(flag[0:1, 0:1], min_val=0, max_val=3 * G)
            with dve.If(spread == 0):
                def add_and_fill(i, b, fill=True):
                    q = i * PER_TILE + b
                    start = dve.value_load(bases[0:1, bass.ds(q + LAG, 1)], min_val=0, max_val=N - 1)
                    if fill:
                        onehots(q + LAG, (b + LAG) % RING)
                    dve.wait_ge(window_free, q + LAG)
                    add_window(dve, q, b, start)

                for q in range(LAG):
                    onehots(q, q)
                with dve.Fori(0, (NT - 1) // 3) as j:
                    for r in range(3):
                        for b in range(PER_TILE):
                            add_and_fill(j * 3, r * PER_TILE + b)
                for b in range(PER_TILE):
                    add_and_fill(NT - 1, b, fill=b + LAG < PER_TILE)
            with dve.Else():
                own_counts = Own(dve, dve_counts)
                own_counts.mark(nc.vector.tensor_scalar(tab_rel[:, :, :], tab_dst[:, :, :], float(W), None, ALU.add))
                with dve.Fori(0, WP) as w:
                    own_counts.wait()
                    kept = own_counts.enter(w, 6)
                    own_counts.done(nc.vector.tensor_scalar(tab_rel[:, :, :], tab_rel[:, :, :], float(-W), None, ALU.add))
                    own_counts.done(nc.vector.tensor_scalar(tab_ok[:, :, :], tab_rel[:, :, :], float(W - 1), None, ALU.is_le))
                    own_counts.done(nc.vector.scalar_tensor_tensor(tab_ok[:, :, :], tab_rel[:, :, :], 0.0, tab_ok[:, :, :], ALU.is_ge, ALU.mult))
                    own_counts.done(nc.vector.scalar_tensor_tensor(tab_to[:, :, :], tab_high[:, :, :], float(W), tab_rel[:, :, :], ALU.mult, ALU.add))
                    own_counts.done(nc.vector.scalar_tensor_tensor(tab_to[:, :, :], tab_to[:, :, :], 1.0, tab_ok[:, :, :], ALU.add, ALU.mult))
                    for c in range(2):
                        last = nc.vector.tensor_scalar(tab_win[:, :, :, c].rearrange("p g t -> p t g"), tab_to[:, :, :], -1.0, None, ALU.add)
                    own_counts.mark(last)
                    with dve.Fori(0, G // RING) as j:
                        own_counts.wait()
                        for b in range(RING):
                            onehots(j * RING + b, b)
                        for b in range(RING):
                            q = w * G + j * RING + b
                            dve.wait_ge(window_free, q + LAG)
                            add_window(dve, q, b, w * W)
                    own_counts.leave(kept, WP)
            nc.vector.memset(small[:, 0:1], 0.0).then_inc(countsT_ready, 1)

            dve.memset(stat[:, 7:8], 0.0).then_inc(LAYER[0]["msgs_out"], 1)
            dve.wait_ge(h_free, 2 * NT + 2)
            dve_slope(0)
            put_counts(dve, EARLY)
            dve.wait_ge(early_put, 2 * EARLY + 1)
            dve_args(0, 0, own)
            put_counts(dve, EARLY + 1)
            dve_numerators(0, 0, own)
            put_counts(dve, EARLY + 2)
            dve.wait_ge(w2_in, 16 * KC)
            dve.wait_ge(att2_in, 32)
            for n in range(ACT_COLUMNS, ACT_COLUMNS + DVE_COLUMNS):
                attention_column(n, own)
            dve_attention(0, own)
            for s in range(0, NT, 2):
                dve.wait_ge(split_hi, s + 1)
                nc.vector.tensor_tensor(H[1][:, s, :], h_next[:, s, :], H[0][:, s, :].bitcast(F32), ALU.subtract).then_inc(split_dve, 1)
            dve_attention(1, own)
            dve_ffn(dve, own)

            for i in range(NT):
                if i + 1 < NT:
                    turned_low(i + 1)
                dve.wait_ge(proj_done, i + 1)
                dve.wait_ge(x2_plus, i + 1)
                if i >= 2:
                    dve.wait_ge(out_stored[i % 2], 32 * (i // 2))
                b = 4 + 2 * (i % 2)
                dve.tensor_tensor(out_sb[:, i % 2, :], PS[0:T, b:b + 2, :].rearrange("p b c -> p (b c)")[:, 0:D], x2_rows(i), ALU.add).then_inc(out_ready, 1)

        @block.tensor
        def _(pe):
            pe.wait_ge(consts_ready, 3)
            pe.wait_ge(edge_rows_ready, 1)
            for b, rows in enumerate((src_low, win, dst_f, src_high)):
                for t in range(ET):
                    nc.tensor.transpose(PS[0:T, b, t * G:(t + 1) * G], rows[:, t * T:(t + 1) * T], ident[0:G, 0:G])
            nc.tensor.matmul(bank(4, 1, 1), small[0:G, 4:5], ones[0:G, 0:1], start=True, stop=True).then_inc(edge_rows_turned, 1)

            def turn_rows(i):
                pe.wait_ge(xn_ready, i + 1)
                if not isinstance(i, int) or i >= 1:
                    pe.wait_ge(xt_raw_ready, i)
                for k in range(KC):
                    last = nc.tensor.transpose(blocks(0, KC)[:, k, 0:T], xn[:, k * P:(k + 1) * P], ident[0:T, 0:T])
                last.then_inc(xn_turned, 1)

            def messages(i, part=0, parts=1):
                todo = [(h, n) for h in range(2) for n in range(3 * KC)]
                size = len(todo) // parts
                for h, n in todo[part * size:(part + 1) * size]:
                    if (h, n) == (0, 0):
                        pe.wait_ge(w_lo_ready, 2)
                        pe.wait_ge(xt_hi_ready, i + 1)
                    if n == 0:
                        pe.wait_ge(h_free, 2 * i + 1 + h)
                    if (h, n) == (0, 2 * KC):
                        pe.wait_ge(xt_lo_ready, i + 1)
                    lo, hi = ((0, HALF), (HALF, WX))[h]
                    (a, b), k = HIGH_FIRST[n // KC], n % KC
                    last = nc.tensor.matmul(bank(5 + h, T, hi - lo), XT[a][:, k, :], Wg[b][:, k, lo:hi], start=(n == 0), stop=(n == 3 * KC - 1))
                    if n == 3 * KC - 1:
                        last.then_inc(h_done, 1)

            def count(q, buf):
                pe.wait_ge(onehots_ready, q + 2)
                pe.wait_ge(window_free, q + 2)
                for t in range(ET):
                    last = nc.tensor.matmul(bank(WINDOW_BANKS[buf % 2], T, NT * W), oh_src[:, buf, t, 0:T], oh_win[:, buf, t, :], start=(t == 0), stop=(t == ET - 1))
                last.then_inc(group_counted, 1)

            def turn_counts(d, h):
                pe.wait_ge(early_conv, d + 1)
                pe.wait_ge(early_put, 2 * d + 1 + h)
                for s in range(NT // 2):
                    last = nc.tensor.transpose(blocks(3, NT // 2)[0:T, s, 0:T], ct_early[:, h * NT // 2 + s, :], ident[0:T, 0:T])
                last.then_inc(early_turned, 1)

            pe.wait_ge(tables_ready, 1)
            spread = pe.value_load(flag[0:1, 0:1], min_val=0, max_val=3 * G)
            with pe.If(spread == 0):
                def count_and_multiply(i, last=False, early=False):
                    for b in range(PER_TILE):
                        count(i * PER_TILE + b, b % RING)
                        if b == PER_TILE - 2 and not last:
                            turn_rows(i + 1)
                        if b in (0, 4) and early:
                            turn_counts(i - 3, b // 4)
                        if b >= PER_TILE - SHARES:
                            messages(i, b - (PER_TILE - SHARES), SHARES)

                turn_rows(0)
                with pe.Fori(0, 3) as i:
                    count_and_multiply(i)
                with pe.Fori(3, NT - 1) as i:
                    count_and_multiply(i, early=True)
                count_and_multiply(NT - 1, last=True, early=True)
            with pe.Else():
                with pe.Fori(0, WP) as w:
                    with pe.Fori(0, G // RING) as j:
                        for b in range(RING):
                            count(w * G + j * RING + b, b)
                pe.wait_ge(countsT_ready, 1)
                turn_rows(0)
                with pe.Fori(0, 3) as i:
                    messages(i)
                    turn_rows(i + 1)
                with pe.Fori(3, NT - 1) as i:
                    turn_counts(i - 3, 0)
                    messages(i)
                    turn_counts(i - 3, 1)
                    turn_rows(i + 1)
                turn_counts(NT - 4, 0)
                messages(NT - 1)
                turn_counts(NT - 4, 1)
            pe.wait_ge(h_free, 2 * NT + 2)
            pe.wait_ge(countsT_ready, 1)
            pe.wait_ge(early_put, 2 * EARLY + 1)
            pe_terms(0)
            for d in range(EARLY, NT):
                pe.wait_ge(ct_conv, d - EARLY + 1)
                if d == EARLY + 1:
                    pe.wait_ge(LAYER[0]["asb_ready"], 1)
                if d == EARLY + 2:
                    pe.wait_ge(counts_ready, 1)
                for s in range(NT):
                    last = nc.tensor.transpose(blocks(3 * (d % 2), NT)[0:T, s, 0:T], ct_f[:, d % 2, s, :], ident[0:T, 0:T])
                last.then_inc(ct_turned, 1)
            pe.wait_ge(counts_ready, 2)
            pe_attention(0)
            pe_attention(1)
            pe_ffn(pe)

            def project(i):
                pe.wait_ge(yt_lo, i + 1)
                if i >= 2:
                    pe.wait_ge(out_ready, i - 1)
                b = 4 + 2 * (i % 2)
                to = PS[0:T, b:b + 2, :].rearrange("p b c -> p (b c)")
                for slot in range(3):
                    for m in range(3 * KC):
                        (x_, y_), k = PARTS[m // KC], m % KC
                        last = pe.matmul(to[:, slot * WB:(slot + 1) * WB], yT[x_][:, i % 2, k, :], Ws[y_][slot][:, k, 0:WB], start=(m == 0), stop=(m == 3 * KC - 1))
                last.then_inc(proj_done, 1)

            pe.wait_ge(ws_lo, BLOCKS + 3)
            pe.wait_ge(group_free, len(USE))
            for i in range(NT):
                if i + 1 < NT:
                    turn_last(i + 1)
                project(i)


_INS = ("x", "src", "dst", "L0_gnn_W1", "L0_gnn_att_src1", "L0_gnn_att_dst1", "L0_gnn_b1", "L0_gnn_W2", "L0_gnn_att_src2",
        "L0_gnn_att_dst2", "L0_gnn_b2", "L0_ffn_Wqk", "L0_ffn_bqk", "L0_ffn_Wv", "L0_ffn_bv", "L0_ffn_conv_w", "L0_ffn_conv_b",
        "L0_ffn_glob", "L0_ffn_pos_bias", "L0_ffn_Wg1", "L0_ffn_bg1", "L0_ffn_Wg2", "L0_ffn_bg2", "L0_ffn_Wp", "L0_ffn_bp")


def kernel(**inputs):
    import numpy as _np
    import concourse.bacc as _bacc
    from concourse import mybir as _mybir
    from concourse.bass_utils import run_bass_kernel_spmd as _run

    nc = _bacc.Bacc("TRN2", target_bir_lowering=False, num_devices=1)
    arrays, a = {}, {}
    for name in _INS:
        v = _np.ascontiguousarray(inputs[name])
        arrays[f"in_{name}_dram"] = v
        a[name] = nc.dram_tensor(f"in_{name}_dram", v.shape, _mybir.dt.from_np(v.dtype), kind="ExternalInput").ap()
    out = nc.dram_tensor("out_dram", (N, D), F32, kind="ExternalOutput").ap()
    gnn = [{"W": a[f"L0_gnn_W{l}"], "as": a[f"L0_gnn_att_src{l}"], "ad": a[f"L0_gnn_att_dst{l}"], "b": a[f"L0_gnn_b{l}"]} for l in (1, 2)]
    ffn = {name[7:]: a[name] for name in _INS if name.startswith("L0_ffn_")}
    program(nc, a["x"], a["src"], a["dst"], gnn, ffn, out)
    return _run(nc, [arrays], core_ids=[0]).results[0]["out_dram"]
```
